# Optimizing a Trainium2 kernel written in Bass

```python
import numpy as np
import jax
import jax.numpy as jnp

def _softmax(x, axis=-1):
    return jax.nn.softmax(x, axis=axis)

def _gelu(x):
    return jax.nn.gelu(x, approximate=True)

def _silu(x):
    return jax.nn.silu(x)

def _sigmoid(x):
    return jax.nn.sigmoid(x)

def _layernorm(x, axis=-1, eps=1e-05):
    m = jnp.mean(x, axis=axis, keepdims=True)
    v = jnp.var(x, axis=axis, keepdims=True)
    return (x - m) / jnp.sqrt(v + eps)

def _scatter_add(tgt, idx, src, axis=0):
    return tgt.at[idx].add(src)

def _segment_sum(src, seg, n):
    return jax.ops.segment_sum(src, seg, n)
kernel_name = 'mk_gnn_resnorm_d1_gnn_r32_069fb0'

def setup_inputs(seed: int=0):
    np.random.seed(seed)
    _w = jnp.asarray

    def _rec_inputs():
        import jax
        import jax.numpy as jnp
        _gk = jax.random.key(seed)
        x = -0.0003713 + 1 * jax.random.normal(jax.random.fold_in(_gk, 1), (3125, 128), jnp.float32)
        src = jax.random.randint(jax.random.fold_in(_gk, 2), (50000,), 0, 3125, jnp.int32)
        dst = jnp.minimum((3125 * jax.random.uniform(jax.random.fold_in(_gk, 3), (50000,)) ** 2.0).astype(jnp.int32), 99999)
        _o = jnp.argsort(dst, stable=True)
        src = src[_o]
        dst = dst[_o]
        edge_type_16 = jax.random.randint(jax.random.fold_in(_gk, 12), (50000,), 0, 16, jnp.int32)
        return (x, src, dst, edge_type_16)
    x, src, dst, edge_type_16 = _rec_inputs()

    def _L0_gnn_setup():
        import jax, jax.numpy as jnp
        import numpy as np
        N_NODES = 3125
        N_EDGES = 18750
        D_IN = 128
        D_OUT = 128
        N_REL = 16
        N_BASES = 8
        key = jax.random.key(seed)
        ks = jax.random.split(key, 6)
        x = jax.random.normal(ks[0], (N_NODES, D_IN), dtype=jnp.float32)
        edge_index = jax.random.randint(ks[1], (2, N_EDGES), 0, N_NODES, dtype=jnp.int64)
        edge_type = jax.random.randint(ks[2], (N_EDGES,), 0, N_REL, dtype=jnp.int64)
        b_lim = float(np.sqrt(6.0 / (D_IN + D_OUT)))
        c_lim = float(np.sqrt(6.0 / (N_REL + N_BASES)))
        w_lim = float(np.sqrt(6.0 / (D_IN + D_OUT)))
        bases = jax.random.uniform(ks[3], (N_BASES, D_IN, D_OUT), jnp.float32, -b_lim, b_lim)
        coefficients = jax.random.uniform(ks[4], (N_REL, N_BASES), jnp.float32, -c_lim, c_lim)
        w_self = jax.random.uniform(ks[5], (D_OUT, D_IN), jnp.float32, -w_lim, w_lim)
        return {'x': x, 'edge_index': edge_index, 'edge_type': edge_type, 'bases': bases, 'coefficients': coefficients, 'w_self': w_self}
    _L0_gnn_all = _L0_gnn_setup()
    _L0_gnn_in = {k: v for k, v in _L0_gnn_all.items() if k in ('bases', 'coefficients', 'w_self')}
    del _L0_gnn_all
    return {'x': x, 'src': src, 'dst': dst, 'edge_type_16': edge_type_16, 'L0_gnn_bases': _L0_gnn_in['bases'], 'L0_gnn_coefficients': _L0_gnn_in['coefficients'], 'L0_gnn_w_self': _L0_gnn_in['w_self']}

def reference(x, src, dst, edge_type_16, L0_gnn_bases, L0_gnn_coefficients, L0_gnn_w_self):
    import jax
    import jax.numpy as jnp

    def _L0_gnn_ref(x, edge_index, edge_type, bases, coefficients, w_self):
        import jax, jax.numpy as jnp
        import numpy as np
        N_NODES = 3125
        N_EDGES = 18750
        D_IN = 128
        D_OUT = 128
        N_REL = 16
        N_BASES = 8
        out = x @ w_self.T
        weights = jnp.einsum('rb,bio->rio', coefficients, bases)
        row, col = (edge_index[0], edge_index[1])
        xc = x[col]
        n_rel = weights.shape[0]
        msg = jnp.zeros((xc.shape[0], w_self.shape[0]), dtype=x.dtype)
        for r in range(n_rel):
            sel = (edge_type == r)[:, None]
            msg = msg + jnp.where(sel, xc @ weights[r], jnp.zeros((), x.dtype))
        out = out.at[row].add(msg)
        return out
    edge_index = jnp.stack([src, dst])
    x = _layernorm(x + _L0_gnn_ref(x, edge_index, edge_type_16, L0_gnn_bases, L0_gnn_coefficients, L0_gnn_w_self), axis=-1)
    return x

_drawn_inputs = setup_inputs


def setup_inputs(seed=0):
    import zlib

    import numpy as np

    out = dict(_drawn_inputs(seed))
    spreads = {}
    factors = {}
    for name, (base, spread) in spreads.items():
        noise = np.random.default_rng([zlib.crc32(name.encode()), seed]).standard_normal(out[name].shape)
        drawn = base * np.exp(spread * noise) if base else spread * noise
        out[name] = jnp.asarray(drawn.astype(out[name].dtype))
    for name, factor in factors.items():
        out[name] = (out[name] * factor).astype(out[name].dtype)
    return out
```

```python
from contextlib import ExitStack

import concourse.bass as bass
from concourse import mybir

F32 = mybir.dt.float32
F16 = mybir.dt.float16
BF16 = mybir.dt.bfloat16
I32 = mybir.dt.int32
ALU = mybir.AluOpType
ACT = mybir.ActivationFunctionType
AX_X = mybir.AxisListType.X

P = 128
NODES = 3125
D = 128
TYPES = 16
BASES = 8
EDGES = 50000
EPS = 1e-5

NB = -(-NODES // P)
NFULL = NODES // P
NLAST = NODES - NFULL * P
BLOCK = 256
BLOCKS = -(-NODES // BLOCK)
EP = 125
EJ = EDGES // EP
TILES = (EDGES + BLOCKS * (P - 1)) // P
TP = TILES + TILES % 2
BANK = 512
YCOLS = TYPES * D
YC = YCOLS // BANK

SHIFT = NODES * TYPES * BLOCK // 2
DIGIT = 4096

PLACED = 256
RP = 24
RY = 3
GU = 4
RG = 2 * GU
RH = 8
SU = 4
SCATTER_ROUNDS = (EJ - PLACED) // (2 * SU)


def rgcn(nc, x, src, dst, etype, bases, coefs, w_self, out):
    ctx = ExitStack()
    with ctx:
        def sb(name, shape, dt):
            return ctx.enter_context(nc.sbuf_tensor(name, shape, dt))

        def sem(name):
            return ctx.enter_context(nc.semaphore(name))

        table = nc.dram_tensor("table", (NODES * TYPES, D), F32).ap()
        slots = nc.dram_tensor("slots", (P * TP, 1), F32).ap()

        x_sb = sb("x_sb", [P, NB, D], F32)
        xT = sb("xT", [P, NB, P], F32)
        bases_sb = sb("bases_sb", [P, BASES, D], F32)
        coef_bc = sb("coef_bc", [P, TYPES, BASES], F32)
        wself = sb("wself", [P, D], F32)
        wselfT = sb("wselfT", [P, D], F32)
        W = sb("W", [P, TYPES, D], F32)
        W_odd = sb("W_odd", [P, TYPES, D], F32)
        ytile = sb("ytile", [P, RY, YCOLS], F32)

        diag = sb("diag", [P, P], F32)
        ident = sb("ident", [P, P], F32)
        before = sb("before", [P, P], F32)
        ones = sb("ones", [P, P], F32)
        ones_row = sb("ones_row", [P, EJ], F32)
        zeros = sb("zeros", [P, TP], F32)
        iota_slot = sb("iota_slot", [P, P], F16)
        iota_tile = sb("iota_tile", [P, TP], F16)
        iota_row = sb("iota_row", [P, BLOCK], F32)
        iota_t1 = sb("iota_t1", [1, TP], F32)

        src_i = sb("src_i", [EP, EJ], I32)
        dst_i = sb("dst_i", [EP, EJ], I32)
        type_i = sb("type_i", [EP, EJ], I32)
        blk_i = sb("blk_i", [EP, EJ], I32)
        blk_h = sb("blk_h", [EP, EJ], BF16)
        row_i = sb("row_i", [EP, EJ], I32)
        inblk = sb("inblk", [EP, BLOCKS, EJ], BF16)
        rank = sb("rank", [EP, BLOCKS, EJ], F32)
        offs = sb("offs", [EP, BLOCKS], F32)
        need_i = sb("need_i", [P, BLOCKS], I32)
        need_t = sb("need_t", [P, BLOCKS], I32)
        need_f = sb("need_f", [P, BLOCKS], F32)
        ends = sb("ends", [P, BLOCKS], F32)
        starts = sb("starts", [P, BLOCKS], F32)
        pos_f = sb("pos_f", [EP, EJ], F32)
        pos_i = sb("pos_i", [EP, EJ], I32)
        tile_i = sb("tile_i", [EP, EJ], I32)
        slot_i = sb("slot_i", [EP, EJ], I32)
        tile_f = sb("tile_f", [EP, EJ], F32)
        slot_f = sb("slot_f", [EP, EJ], F32)
        addr_i = sb("addr_i", [EP, EJ], I32)
        trow = sb("trow", [EP, EJ], F32)
        word0 = sb("word0", [EP, EJ], F32)
        word1 = sb("word1", [EP, EJ], F32)
        word = sb("word", [EP, EJ], F32)
        wdig_i = sb("wdig_i", [EP, EJ], I32)
        hi_i = sb("hi_i", [EP, EJ], I32)
        lo_i = sb("lo_i", [EP, EJ], I32)
        hi_f = sb("hi_f", [EP, EJ], F32)
        lo_f = sb("lo_f", [EP, EJ], F32)
        tblk_a = sb("tblk_a", [1, TP], F32)
        tblk_b = sb("tblk_b", [1, TP], F32)
        tblk_i = sb("tblk_i", [1, TP], I32)

        slotoh = sb("slotoh", [EP, RP, 2, P], F16)
        tileoh = sb("tileoh", [EP, RP, TP], F16)

        sD = sb("sD", [P, TP], F32)
        sw0 = sb("sw0", [P, TP], F32)
        sw = sb("sw", [P, TP], F32)
        sneg = sb("sneg", [P, TP], F32)
        sval = sb("sval", [P, TP], I32)
        sidx = sb("sidx", [P, TP], I32)
        srow_i = sb("srow_i", [P, TP], I32)
        sempty = sb("sempty", [P, TP], F32)
        srow = sb("srow", [P, TP], F32)

        gath = sb("gath", [P, 2, GU, D], F32)
        idx_ring = sb("idx_ring", [P, 2, GU], I32)
        addr_ring = sb("addr_ring", [EP, 2, SU], I32)
        word_ring = sb("word_ring", [EP, 2, SU], F32)
        rowoh = sb("rowoh", [P, RH, BLOCK], F32)

        h = ytile[:, :, :].rearrange("p s c -> p (s c)")[:, 0:NB * D].rearrange("p (q f) -> p q f", q=NB)
        hc = xT
        sq = sb("sq", [P, D], F32)
        hsum = sb("hsum", [P, NB], F32)
        hmean = sb("hmean", [P, NB], F32)
        hvar = sb("hvar", [P, NB], F32)
        hstd = sb("hstd", [P, NB], F32)
        hinv = sb("hinv", [P, NB], F32)
        eps_c = sb("eps_c", [P, 1], F32)

        ps = ctx.enter_context(nc.psum_tensor("ps", [P, 8, BANK], F32))
        acc = ps[:, 0:7, :].rearrange("p b c -> p (b c)")
        ps_hi, ps_lo = ps[:, 4, 0:TP], ps[:, 5, 0:TP]
        ps_before, ps_total = ps[0:EP, 7, 0:BLOCKS], ps[:, 7, BLOCKS:2 * BLOCKS]

        x_loaded = sem("x_loaded")
        bases_loaded = sem("bases_loaded")
        coef_loaded = sem("coef_loaded")
        wself_loaded = sem("wself_loaded")
        src_loaded = sem("src_loaded")
        dst_loaded = sem("dst_loaded")
        consts = sem("consts")
        pool_step = sem("pool_step")
        dve_step = sem("dve_step")
        zero_ready = sem("zero_ready")
        slots_zeroed = sem("slots_zeroed")
        masks = sem("masks")
        xT_made = sem("xT_made")
        xT_copied = sem("xT_copied")
        w_ready = sem("w_ready")
        y_made = sem("y_made")
        y_copied = sem("y_copied")
        y_stored = [sem(f"y_stored{i}") for i in range(RY)]
        ranks_ready = sem("ranks_ready")
        prefix_ready = sem("prefix_ready")
        addr_ready = sem("addr_ready")
        scattered = [sem(f"scattered{i}") for i in range(2)]
        addr_copied = sem("addr_copied")
        idx_copied = sem("idx_copied")
        place_ready = sem("place_ready")
        place_used = sem("place_used")
        slots_loaded = sem("slots_loaded")
        sidx_ready = sem("sidx_ready")
        decoded = sem("decoded")
        tblk_ready = sem("tblk_ready")
        gathered = [sem(f"gathered{i}") for i in range(RG)]
        rowoh_ready = sem("rowoh_ready")
        summed = sem("summed")
        centred = sem("centred")
        squared = sem("squared")
        std_ready = sem("std_ready")
        normed = sem("normed")
        out_stored = sem("out_stored")

        block = ctx.enter_context(nc.Block())

        CONSTS = 5

        def edge_pieces():
            return [(0, 112), (112, 124), (124, EP)]

        @block.sync
        def _(sp):
            def load_edges(tile, a, s):
                v = a.rearrange("(p j) -> p j", p=EP)
                for lo, hi in edge_pieces():
                    sp.dma_start(tile[lo:hi, :], v[lo:hi, :]).then_inc(s, 16)

            load_edges(src_i, src, src_loaded)
            load_edges(dst_i, dst, dst_loaded)
            load_edges(type_i, etype, dst_loaded)
            sp.wait_ge(zero_ready, 1)
            sp.dma_start(slots.rearrange("(p t) o -> p (t o)", p=P), zeros[:, :]).then_inc(slots_zeroed, 16)

            rows = table.rearrange("(n t) o -> n (t o)", t=TYPES)
            with sp.Fori(0, NFULL // RY) as g:
                for s in range(RY):
                    q = g * RY + s
                    sp.wait_ge(y_copied, YC * (q + 1))
                    sp.dma_start(rows[bass.ds(q * P, P), :], ytile[:, s, :]).then_inc(y_stored[s], 16)
            sp.wait_ge(y_copied, YC * NB)
            sp.dma_start(rows[NFULL * P:NODES, :], ytile[0:NLAST, NFULL % RY, :]).then_inc(y_stored[NFULL % RY], 16)

            for half in range(2):
                sp.wait_ge(scattered[half], 16 * SU * SCATTER_ROUNDS)
            sp.dma_start(sD[:, :], slots.rearrange("(p t) o -> p (t o)", p=P)).then_inc(slots_loaded, 16)

            sp.wait_ge(normed, 1)
            sp.dma_start(out[0:NFULL * P, :].rearrange("(q p) f -> p q f", p=P), h[:, 0:NFULL, :]).then_inc(out_stored, 16)
            sp.dma_start(out[NFULL * P:NODES, :], h[0:NLAST, NFULL, :]).then_inc(out_stored, 16)
            sp.wait_ge(out_stored, 32)

        @block.gpsimd
        def _(pool):
            nc.gpsimd.iota(diag[:, :], [[1, P]], channel_multiplier=-1,
                           allow_small_or_imprecise_dtypes=True).then_inc(consts, 1)
            nc.gpsimd.iota(iota_slot[:, :], [[1, P]], channel_multiplier=0,
                           allow_small_or_imprecise_dtypes=True).then_inc(consts, 1)
            nc.gpsimd.iota(iota_tile[:, :], [[1, TP]], channel_multiplier=0,
                           allow_small_or_imprecise_dtypes=True).then_inc(consts, 1)
            nc.gpsimd.iota(iota_row[:, :], [[1, BLOCK]], channel_multiplier=0,
                           allow_small_or_imprecise_dtypes=True).then_inc(consts, 1)
            nc.gpsimd.iota(iota_t1[:, :], [[1, TP]], channel_multiplier=0,
                           allow_small_or_imprecise_dtypes=True).then_inc(consts, 1)


            pool.wait_ge(slots_zeroed, 16)
            pool.wait_ge(addr_ready, 1)

            def scatter_rounds(g, first):
                for half in range(2):
                    j = (g * 2 + half) * SU + PLACED
                    if not first:
                        pool.wait_ge(scattered[half], g * (16 * SU))
                    nc.gpsimd.tensor_copy(addr_ring[:, half, :], addr_i[:, bass.ds(j, SU)]).then_inc(addr_copied, 1)
                    nc.gpsimd.tensor_copy(word_ring[:, half, :], word[:, bass.ds(j, SU)]).then_inc(addr_copied, 1)
                    pool.wait_ge(addr_copied, g * 4 + 2 * (half + 1))
                    nc.gpsimd.nop(nofuse=True)
                    for s in range(SU):
                        nc.gpsimd.indirect_dma_start(
                            out=slots[:, :],
                            out_offset=bass.IndirectOffsetOnAxis(ap=addr_ring[:, half, s:s + 1], axis=0),
                            in_=word_ring[:, half, s:s + 1], in_offset=None).then_inc(scattered[half], 16)

            scatter_rounds(0, True)
            with pool.Fori(1, SCATTER_ROUNDS) as g:
                scatter_rounds(g, False)

            def gather(half, s):
                nc.gpsimd.indirect_dma_start(
                    out=gath[:, half, s, :], out_offset=None, in_=table[:, :],
                    in_offset=bass.IndirectOffsetOnAxis(ap=idx_ring[:, half, s:s + 1], axis=0)
                ).then_inc(gathered[half * GU + s], 16)

            for s in range(RY):
                pool.wait_ge(y_stored[s], 16 * len(range(s, NB, RY)))
            pool.wait_ge(sidx_ready, 1)

            def gather_round(r, half, first, n):
                if not first:
                    pool.wait_ge(summed, (r - 1) * GU)
                nc.gpsimd.tensor_copy(idx_ring[:, half, 0:n], sidx[:, bass.ds(r * GU, n)]).then_inc(idx_copied, 1)
                pool.wait_ge(idx_copied, r + 1)
                nc.gpsimd.nop(nofuse=True)
                for s in range(n):
                    gather(half, s)

            gather_round(0, 0, True, GU)
            gather_round(1, 1, True, GU)
            with pool.Fori(1, TILES // RG) as g:
                for half in range(2):
                    gather_round(g * 2 + half, half, False, GU)
            gather_round(TILES // RG * 2, 0, False, TILES % RG)

        @block.scalar
        def _(act):
            act.dma_start(coef_bc[:, :, :].rearrange("p r b -> p (r b)"),
                          coefs.rearrange("r b -> (r b)").partition_broadcast(P)).then_inc(coef_loaded, 16)
            act.dma_start(bases_sb[:, :, :], bases.rearrange("b i o -> i b o")).then_inc(bases_loaded, 16)
            act.dma_start(wself[:, :], w_self[:, :]).then_inc(wself_loaded, 16)
            act.dma_start(x_sb[:, 0:NFULL, :], x[0:NFULL * P, :].rearrange("(q p) f -> p q f", p=P)).then_inc(x_loaded, 16)
            act.wait_ge(zero_ready, 2)
            act.dma_start(x_sb[0:NLAST, NFULL, :], x[NFULL * P:NODES, :]).then_inc(x_loaded, 16)

            for g in range(-(-NB // 4)):
                n = min(4, NB - 4 * g)
                act.wait_ge(xT_made, g + 1)
                nc.scalar.copy(xT[:, 4 * g:4 * g + n, :].rearrange("p q n -> p (q n)"),
                               ps[:, 6 + g % 2, 0:n * P]).then_inc(xT_copied, 1)
            act.wait_ge(xT_made, -(-NB // 4) + 1)
            nc.scalar.copy(wselfT[:, :], ps[:, 5, 0:P]).then_inc(xT_copied, 1)

            def copy_tile(q, s):
                for c in range(YC):
                    act.wait_ge(y_made, YC * q + c + 1)
                    nc.scalar.copy(ytile[:, s, c * BANK:(c + 1) * BANK], ps[:, c, :]).then_inc(y_copied, 1)

            for q in range(RY):
                copy_tile(q, q)
            with act.Fori(1, NFULL // RY) as g:
                for s in range(RY):
                    act.wait_ge(y_stored[s], 16 * g)
                    copy_tile(g * RY + s, s)
            act.wait_ge(y_stored[NFULL % RY], 16 * (NFULL // RY))
            copy_tile(NFULL, NFULL % RY)

            for q in range(NB):
                act.wait_ge(centred, 1)
                if q:
                    act.wait_ge(squared, q)
                nc.scalar.activation(sq[:, :], hc[:, q, :], ACT.Square,
                                     accum_out=hvar[:, q:q + 1]).then_inc(squared, 1)
            act.wait_ge(squared, NB)
            nc.scalar.activation(hstd[:, :], hvar[:, :], ACT.Sqrt, bias=eps_c[:, 0:1],
                                 scale=1.0 / D).then_inc(std_ready, 1)

        @block.vector
        def _(dve):
            steps = [0]

            def step(ins):
                steps[0] += 1
                ins.then_inc(dve_step, 1)
                dve.wait_ge(dve_step, steps[0])

            nc.vector.memset(zeros[:, :], 0.0).then_inc(zero_ready, 1)
            nc.vector.memset(x_sb[:, NFULL, :], 0.0).then_inc(zero_ready, 1)
            nc.vector.memset(ones_row[:, :], 1.0)
            nc.vector.memset(eps_c[:, :], EPS)
            nc.vector.memset(ones[:, :], 1.0).then_inc(masks, 1)
            dve.wait_ge(consts, CONSTS)
            nc.vector.tensor_scalar(ident[:, :], diag[:, :], 0.0, None, ALU.is_equal).then_inc(masks, 1)
            nc.vector.tensor_scalar(before[:, :], diag[:, :], 0.0, None, ALU.is_gt).then_inc(masks, 1)
            dve.wait_ge(masks, 3)

            dve.wait_ge(coef_loaded, 16)
            dve.wait_ge(bases_loaded, 16)
            for b in range(BASES):
                into, was = (W_odd, W) if b % 2 == 0 else (W, W_odd)
                for r in range(TYPES):
                    if b == 0:
                        last = nc.vector.tensor_scalar(into[:, r, :], bases_sb[:, b, :], coef_bc[:, r, b:b + 1], None, ALU.mult)
                    else:
                        last = nc.vector.scalar_tensor_tensor(into[:, r, :], bases_sb[:, b, :], coef_bc[:, r, b:b + 1],
                                                              was[:, r, :], ALU.mult, ALU.add)
                step(last)
            nc.vector.tensor_copy(hsum[:, 0:1], W[:, 0, 0:1]).then_inc(w_ready, 1)

            dve.wait_ge(src_loaded, 16 * len(edge_pieces()))
            nc.vector.tensor_scalar(row_i[:, :], src_i[:, :], BLOCK - 1, None, ALU.bitwise_and)
            step(nc.vector.tensor_scalar(blk_i[:, :], src_i[:, :], BLOCK.bit_length() - 1, None, ALU.arith_shift_right))
            step(nc.vector.tensor_copy(blk_h[:, :], blk_i[:, :]))
            for k in range(BLOCKS):
                last = nc.vector.tensor_scalar(inblk[:, k, :], blk_h[:, :], float(k), None, ALU.is_equal)
            step(last)
            for k in range(BLOCKS):
                last = nc.vector.tensor_tensor_scan(rank[:, k, :], ones_row[0:EP, :], inblk[:, k, :], 0.0, ALU.mult, ALU.add)
            last.then_inc(ranks_ready, 1)

            dve.wait_ge(dst_loaded, 32 * len(edge_pieces()))
            step(nc.vector.scalar_tensor_tensor(trow[:, :], dst_i[:, :], float(TYPES), type_i[:, :], ALU.mult, ALU.add))
            step(nc.vector.scalar_tensor_tensor(word0[:, :], trow[:, :], float(BLOCK), row_i[:, :], ALU.mult, ALU.add))
            step(nc.vector.tensor_scalar(word1[:, :], word0[:, :], float(-SHIFT), None, ALU.add))
            step(nc.vector.scalar_tensor_tensor(word[:, :], word1[:, :], 0.0, word1[:, :], ALU.is_ge, ALU.add))
            step(nc.vector.tensor_scalar(wdig_i[:, :], word[:, :], float(DIGIT // 2), None, ALU.add))
            nc.vector.tensor_scalar(hi_i[:, :], wdig_i[:, :], DIGIT.bit_length() - 1, None, ALU.arith_shift_right)
            step(nc.vector.tensor_scalar(lo_i[:, :], wdig_i[:, :], DIGIT - 1, None, ALU.bitwise_and))
            nc.vector.tensor_copy(hi_f[:, :], hi_i[:, :])
            nc.vector.tensor_scalar(lo_f[:, :], lo_i[:, :], float(-DIGIT // 2), None, ALU.add)

            dve.wait_ge(prefix_ready, 1)
            step(nc.vector.tensor_scalar(need_i[:, :], ps_total, float(P - 1), None, ALU.add))
            step(nc.vector.tensor_scalar(need_t[:, :], need_i[:, :], P.bit_length() - 1, None, ALU.arith_shift_right))
            step(nc.vector.tensor_copy(need_f[:, :], need_t[:, :]))
            step(nc.vector.tensor_tensor_scan(ends[:, :], ones_row[:, 0:BLOCKS], need_f[:, :], 0.0, ALU.mult, ALU.add))
            step(nc.vector.tensor_tensor(starts[:, :], ends[:, :], need_f[:, :], ALU.subtract))
            step(nc.vector.scalar_tensor_tensor(offs[:, :], starts[0:EP, :], float(P), ps_before, ALU.mult, ALU.add))
            for k in range(BLOCKS):
                last = nc.vector.scalar_tensor_tensor(rank[:, k, :], rank[:, k, :], offs[:, k:k + 1], inblk[:, k, :],
                                                      ALU.add, ALU.mult)
            step(last)
            step(nc.vector.tensor_reduce(pos_f[:, :], rank[:, :, :].rearrange("p k j -> p j k"), AX_X, ALU.add))
            step(nc.vector.tensor_scalar(pos_i[:, :], pos_f[:, :], -1.0, None, ALU.add))
            nc.vector.tensor_scalar(tile_i[:, :], pos_i[:, :], P.bit_length() - 1, None, ALU.arith_shift_right)
            step(nc.vector.tensor_scalar(slot_i[:, :], pos_i[:, :], P - 1, None, ALU.bitwise_and))
            nc.vector.scalar_tensor_tensor(addr_i[:, :], slot_i[:, :], float(TP), tile_i[:, :], ALU.mult, ALU.add).then_inc(addr_ready, 1)
            nc.vector.tensor_copy(tile_f[:, :], tile_i[:, :])
            step(nc.vector.tensor_copy(slot_f[:, :], slot_i[:, :]))

            def place(j, s):
                nc.vector.tensor_scalar(slotoh[:, s, 0, :], iota_slot[0:EP, :], slot_f[:, bass.ds(j, 1)], hi_f[:, bass.ds(j, 1)],
                                        ALU.is_equal, ALU.mult)
                nc.vector.tensor_scalar(slotoh[:, s, 1, :], iota_slot[0:EP, :], slot_f[:, bass.ds(j, 1)], lo_f[:, bass.ds(j, 1)],
                                        ALU.is_equal, ALU.mult)
                nc.vector.tensor_scalar(tileoh[:, s, :], iota_tile[0:EP, :], tile_f[:, bass.ds(j, 1)], None,
                                        ALU.is_equal).then_inc(place_ready, 1)

            for j in range(RP):
                place(j, j)
            with dve.Fori(1, PLACED // RP) as g:
                for s in range(RP):
                    j = g * RP + s
                    dve.wait_ge(place_used, j - (RP - 1))
                    place(j, s)
            for j in range(PLACED // RP * RP, PLACED):
                dve.wait_ge(place_used, j - (RP - 1))
                place(j, j % RP)

            dve.wait_ge(place_used, PLACED)
            dve.wait_ge(slots_loaded, 16)
            step(nc.vector.scalar_tensor_tensor(sw0[:, :], ps_hi, float(DIGIT), sD[:, :], ALU.mult, ALU.add))
            step(nc.vector.tensor_tensor(sw[:, :], ps_lo, sw0[:, :], ALU.add))
            step(nc.vector.scalar_tensor_tensor(sneg[:, :], sw[:, :], 0.0, sw[:, :], ALU.is_gt, ALU.subtract))
            step(nc.vector.tensor_scalar(sval[:, :], sneg[:, :], -1.0, float(SHIFT), ALU.mult, ALU.add))
            nc.vector.tensor_scalar(sidx[:, :], sval[:, :], BLOCK.bit_length() - 1, None,
                                    ALU.arith_shift_right).then_inc(sidx_ready, 1)
            nc.vector.tensor_scalar(sempty[:, :], sw[:, :], 0.0, float(2 * BLOCK), ALU.is_equal, ALU.mult)
            step(nc.vector.tensor_scalar(srow_i[:, :], sval[:, :], BLOCK - 1, None, ALU.bitwise_and))
            step(nc.vector.tensor_tensor(srow[:, :], srow_i[:, :], sempty[:, :], ALU.add))

            def row_onehot(t, s):
                nc.vector.tensor_scalar(rowoh[:, s, :], iota_row[:, :], srow[:, bass.ds(t, 1)], None,
                                        ALU.is_equal).then_inc(rowoh_ready, 1)

            for t in range(2):
                row_onehot(t, t)
            step(nc.vector.tensor_scalar(tblk_a[:, :], iota_t1[:, :], ends[0:1, 0:1], None, ALU.is_ge))
            now, other = tblk_a, tblk_b
            for k in range(1, BLOCKS - 1):
                step(nc.vector.scalar_tensor_tensor(other[:, :], iota_t1[:, :], ends[0:1, k:k + 1], now[:, :], ALU.is_ge, ALU.add))
                now, other = other, now
            nc.vector.tensor_scalar(tblk_i[:, :], now[:, :], float(BLOCK), None, ALU.mult).then_inc(tblk_ready, 1)

            for t in range(2, RH):
                row_onehot(t, t)
            with dve.Fori(1, TILES // RH) as g:
                for s in range(RH):
                    t = g * RH + s
                    dve.wait_ge(summed, t - (RH - 1))
                    row_onehot(t, s)
            for t in range(TILES // RH * RH, TILES):
                dve.wait_ge(summed, t - (RH - 1))
                row_onehot(t, t % RH)

            dve.wait_ge(summed, TILES)
            dve.wait_ge(x_loaded, 32)
            flat = "p q f -> p (q f)"
            step(nc.vector.tensor_tensor(h[:, :, :].rearrange(flat), acc[:, 0:NB * D], x_sb[:, :, :].rearrange(flat), ALU.add))
            step(nc.vector.tensor_reduce(hsum[:, :], h[:, :, :], AX_X, ALU.add))
            step(nc.vector.tensor_scalar(hmean[:, :], hsum[:, :], 1.0 / D, None, ALU.mult))
            nc.vector.tensor_tensor(hc[:, :, :], h[:, :, :], hmean[:, :].unsqueeze(2).broadcast_to([P, NB, D]),
                                    ALU.subtract).then_inc(centred, 1)
            dve.wait_ge(std_ready, 1)
            step(nc.vector.reciprocal(hinv[:, :], hstd[:, :]))
            dve.wait_ge(centred, 1)
            nc.vector.tensor_tensor(h[:, :, :], hc[:, :, :], hinv[:, :].unsqueeze(2).broadcast_to([P, NB, D]),
                                    ALU.mult).then_inc(normed, 1)

        @block.tensor
        def _(pe):
            pe.wait_ge(masks, 3)
            pe.wait_ge(x_loaded, 32)
            for g in range(-(-NB // 4)):
                n = min(4, NB - 4 * g)
                if g >= 2:
                    pe.wait_ge(xT_copied, g - 1)
                for i in range(n):
                    last = nc.tensor.transpose(ps[:, 6 + g % 2, i * P:(i + 1) * P], x_sb[:, 4 * g + i, :], ident[:, :])
                last.then_inc(xT_made, 1)
            pe.wait_ge(wself_loaded, 16)
            nc.tensor.transpose(ps[:, 5, 0:P], wself[:, :], ident[:, :]).then_inc(xT_made, 1)

            def prefix():
                pe.wait_ge(xT_copied, -(-NB // 4))
                pe.wait_ge(ranks_ready, 1)
                nc.tensor.matmul(ps_before, before[0:EP, 0:EP], rank[:, :, EJ - 1], start=True, stop=True)
                nc.tensor.matmul(ps_total, ones[0:EP, :], rank[:, :, EJ - 1], start=True, stop=True).then_inc(prefix_ready, 1)

            def table_tile(q, first):
                for c in range(YC):
                    if not first:
                        pe.wait_ge(y_copied, YC * q + c - (YC - 1))
                    nc.tensor.matmul(ps[:, c, :], xT[:, q, :],
                                     W[:, c * 4:(c + 1) * 4, :].rearrange("p r o -> p (r o)"),
                                     start=True, stop=True).then_inc(y_made, 1)

            EARLY = 10
            pe.wait_ge(xT_copied, -(-NB // 4) + 1)
            pe.wait_ge(w_ready, 1)
            for q in range(NB):
                if q == EARLY:
                    prefix()
                table_tile(q, q == 0)

            def place(j, s, first, last):
                pe.wait_ge(place_ready, j + 1)
                nc.tensor.matmul(ps_hi, slotoh[:, s, 0, :], tileoh[:, s, :], start=first, stop=last, skip_group_check=True)
                nc.tensor.matmul(ps_lo, slotoh[:, s, 1, :], tileoh[:, s, :], start=first, stop=last,
                                 skip_group_check=True).then_inc(place_used, 1)

            for j in range(RP):
                place(j, j, j == 0, False)
            with pe.Fori(1, PLACED // RP) as g:
                for s in range(RP):
                    place(g * RP + s, s, False, False)
            for j in range(PLACED // RP * RP, PLACED):
                place(j, j % RP, False, j == PLACED - 1)

            pe.wait_ge(sidx_ready, 1)
            pe.wait_ge(y_copied, YC * NB)
            for q in range(NB):
                nc.tensor.matmul(acc[:, q * P:(q + 1) * P], xT[:, q, :], wselfT[:, :], start=(q % 4 == 0), stop=False,
                                 skip_group_check=True)

            def add_tile(g, s):
                t = g * RG + s
                col = pe.value_load(tblk_i[0:1, bass.ds(t, 1)], min_val=0, max_val=(BLOCKS - 1) * BLOCK)
                pe.wait_ge(rowoh_ready, t + 1)
                pe.wait_ge(gathered[s], 16 * (g + 1))
                for c in range(BLOCK // P):
                    last = nc.tensor.matmul(acc[:, bass.ds(col + c * P, P)], rowoh[:, s, c * P:(c + 1) * P],
                                            gath[:, s // GU, s % GU, :], start=False, stop=False, skip_group_check=True)
                last.then_inc(summed, 1)

            pe.wait_ge(tblk_ready, 1)
            with pe.Fori(0, TILES // RG) as g:
                for s in range(RG):
                    add_tile(g, s)
            for s in range(TILES % RG):
                add_tile(TILES // RG, s)


def kernel(x, src, dst, edge_type_16, L0_gnn_bases, L0_gnn_coefficients, L0_gnn_w_self):
    import numpy as np
    import concourse.bacc as bacc
    from concourse.bass_utils import run_bass_kernel_spmd

    nc = bacc.Bacc("TRN2", target_bir_lowering=False, num_devices=1)
    named = dict(x=x, src=src, dst=dst, etype=edge_type_16, bases=L0_gnn_bases, coefs=L0_gnn_coefficients,
                 w_self=L0_gnn_w_self)
    arrays, args = {}, []
    for name, a in named.items():
        a = np.ascontiguousarray(a)
        arrays[f"in_{name}"] = a
        args.append(nc.dram_tensor(f"in_{name}", a.shape, mybir.dt.from_np(a.dtype), kind="ExternalInput").ap())
    out = nc.dram_tensor("out_0", (NODES, D), F32, kind="ExternalOutput").ap()
    rgcn(nc, *args, out)
    r = run_bass_kernel_spmd(nc, [arrays], core_ids=[0])
    return r.results[0]["out_0"]
```

```python
from contextlib import ExitStack

import concourse.bass as bass
from concourse import mybir

F32 = mybir.dt.float32
F16 = mybir.dt.float16
BF16 = mybir.dt.bfloat16
I32 = mybir.dt.int32
ALU = mybir.AluOpType
ACT = mybir.ActivationFunctionType
AX_X = mybir.AxisListType.X

P = 128
NODES = 3125
D = 128
TYPES = 16
BASES = 8
EDGES = 50000
EPS = 1e-5

NB = -(-NODES // P)
XG = -(-NB // 4)
WARM = (12, 10)
NFULL = NODES // P
NLAST = NODES - NFULL * P
BLOCK = 256
BLOCKS = -(-NODES // BLOCK)
EP = 125
EJ = EDGES // EP
TILES = (EDGES + BLOCKS * (P - 1)) // P
TP = TILES + TILES % 2
BANK = 512
YCOLS = TYPES * D
YC = YCOLS // BANK

SHIFT = NODES * TYPES * BLOCK // 2
DIGIT = 4096

RY = 4
RP = 16
PC = RP // YC
DVE_DIGITS = (1, 3, 5, 9, 11, 13)
ACT_DIGITS = [v for v in range(RP) if v not in DVE_DIGITS]
EARLY = 10
GROUPS = NB - EARLY
TRAIL = 10
PLACED = GROUPS * RP + TRAIL
SU = 15
SCATTER_ROUNDS = (EJ - PLACED) // (2 * SU)
assert SCATTER_ROUNDS * 2 * SU == EJ - PLACED
GU = 8
RG = 2 * GU
IC = P // BASES
IH = D // IC


def rgcn(nc, x, src, dst, etype, bases, coefs, w_self, out):
    ctx = ExitStack()
    with ctx:
        def sb(name, shape, dt):
            return ctx.enter_context(nc.sbuf_tensor(name, shape, dt))

        def sem(name):
            return ctx.enter_context(nc.semaphore(name))

        weights = nc.dram_tensor("weights", (TYPES, D, D), F32).ap()
        table = nc.dram_tensor("table", (NODES * TYPES, D), F32).ap()
        slots = nc.dram_tensor("slots", (P * TP, 1), F32).ap()

        x_sb = sb("x_sb", [P, NB, D], F32)
        xT = sb("xT", [P, NB, P], F32)
        bases_sb = sb("bases_sb", [P, IH, D], F32)
        coef_bc = sb("coef_bc", [P, TYPES, BASES], F32)
        own_i = sb("own_i", [P, BASES], I32)
        own_s = sb("own_s", [P, BASES], I32)
        own = sb("own", [P, BASES], F32)
        same_i = sb("same_i", [P, IC], I32)
        same_m = sb("same_m", [P, IC], I32)
        same = sb("same", [P, IC], F32)
        coef_own = sb("coef_own", [P, TYPES, BASES], F32)
        coef_col = sb("coef_col", [P, TYPES], F32)
        mix = sb("mix", [P, TYPES, IC], F32)
        xcur = sb("xcur", [P, 2, P], F32)
        wself = sb("wself", [P, D], F32)
        wselfT = sb("wselfT", [P, D], F32)
        W = sb("W", [P, TYPES, D], F32)
        ytile = sb("ytile", [P, RY, YCOLS], F32)
        wmix = ytile[:, RY - 1, :].rearrange("p (a c) -> p a c", a=2)

        diag = sb("diag", [P, P], F32)
        ident = sb("ident", [P, P], F32)
        before = sb("before", [P, P], F32)
        ones = sb("ones", [P, P], F32)
        ones_row = sb("ones_row", [P, EJ], F32)
        zeros = sb("zeros", [P, TP], F32)
        iota_slot = sb("iota_slot", [P, P], F16)
        iota_tile = sb("iota_tile", [P, TP], F16)
        iota_row = sb("iota_row", [P, BLOCK], F32)
        iota_t1 = sb("iota_t1", [1, TP], F32)

        src_i = sb("src_i", [EP, EJ], I32)
        dst_i = sb("dst_i", [EP, EJ], I32)
        type_i = sb("type_i", [EP, EJ], I32)
        blk_i = sb("blk_i", [EP, EJ], I32)
        blk_h = sb("blk_h", [EP, EJ], BF16)
        row_i = sb("row_i", [EP, EJ], I32)
        inblk = sb("inblk", [EP, BLOCKS, EJ], BF16)
        rank_all = sb("rank", [P, BLOCKS, EJ], F32)
        rank = rank_all[0:EP, :, :]
        offs = sb("offs", [EP, BLOCKS], F32)
        need_i = sb("need_i", [P, BLOCKS], I32)
        need_t = sb("need_t", [P, BLOCKS], I32)
        need_f = sb("need_f", [P, BLOCKS], F32)
        ends = sb("ends", [P, BLOCKS], F32)
        starts = sb("starts", [P, BLOCKS], F32)
        pos_f = sb("pos_f", [EP, EJ], F32)
        pos_i = sb("pos_i", [EP, EJ], I32)
        tile_i = sb("tile_i", [EP, EJ], I32)
        slot_i = sb("slot_i", [EP, EJ], I32)
        tile_f = sb("tile_f", [EP, EJ], F32)
        slot_f = sb("slot_f", [EP, EJ], F32)
        addr_i = sb("addr_i", [EP, EJ], I32)
        word0 = sb("word0", [EP, EJ], F32)
        word1 = sb("word1", [EP, EJ], F32)
        word = sb("word", [EP, EJ], F32)
        wdig_i = sb("wdig_i", [EP, EJ], I32)
        hi_i = sb("hi_i", [EP, EJ], I32)
        lo_i = sb("lo_i", [EP, EJ], I32)
        hi_f = sb("hi_f", [EP, EJ], F32)
        lo_f = sb("lo_f", [EP, EJ], F32)
        tblk_a = sb("tblk_a", [1, TP], F32)
        tblk_b = sb("tblk_b", [1, TP], F32)
        tblk_i = sb("tblk_i", [1, TP], I32)
        ends_i = sb("ends_i", [1, BLOCKS], I32)
        dst_w = sb("dst_w", [EP, EJ], F32)
        type_w = sb("type_w", [EP, EJ], F32)
        row_w = sb("row_w", [EP, EJ], F32)
        word_pos = sb("word_pos", [EP, EJ], F32)

        zeros_h = sb("zeros_h", [P, TP], F16)
        oneslot = sb("oneslot", [EP, RP, P], F16)
        slotoh = sb("slotoh", [EP, RP, 2, P], F16)
        tileoh = sb("tileoh", [EP, RP, TP], F16)

        sD = sb("sD", [P, TP], F32)
        sw0 = sb("sw0", [P, TP], F32)
        sw = sb("sw", [P, TP], F32)
        sneg = sb("sneg", [P, TP], F32)
        sval = sb("sval", [P, TP], I32)
        sidx = sb("sidx", [P, TP], I32)
        srow_i = sb("srow_i", [P, TP], I32)
        sempty = sb("sempty", [P, TP], F32)
        srow = sb("srow", [P, TP], F32)

        gath = sb("gath", [P, 2, GU, D], F32)
        idx_ring = sb("idx_ring", [P, 2, GU], I32)
        addr_ring = sb("addr_ring", [EP, 2, SU], I32)
        word_ring = sb("word_ring", [EP, 2, SU], F32)
        rowoh = rank_all[:, :, :].rearrange("p k j -> p (k j)")[:, 0:RG * BLOCK].rearrange("p (t r) -> p t r", t=RG)

        in_ytile = ytile[:, :, :].rearrange("p s c -> p (s c)")
        h = in_ytile[:, 0:NB * D].rearrange("p (q f) -> p q f", q=NB)
        normal = in_ytile[:, NB * D:2 * NB * D].rearrange("p (q f) -> p q f", q=NB)
        sq = sb("sq", [P, 4, D], F32)
        hsum = sb("hsum", [P, NB], F32)
        hneg = sb("hneg", [P, NB], F32)
        hvar = sb("hvar", [P, NB], F32)
        hstd = sb("hstd", [P, NB], F32)
        hinv = sb("hinv", [P, NB], F32)
        eps_c = sb("eps_c", [P, 1], F32)

        ps = ctx.enter_context(nc.psum_tensor("ps", [P, 8, BANK], F32))
        acc = ps[:, 0:7, :].rearrange("p b c -> p (b c)")
        ps_hi, ps_lo = ps[:, 4, 0:TP], ps[:, 5, 0:TP]
        ps_before, ps_total = ps[0:EP, 7, 0:BLOCKS], ps[:, 7, BLOCKS:2 * BLOCKS]

        x_loaded = sem("x_loaded")
        bases_loaded = sem("bases_loaded")
        coef_loaded = sem("coef_loaded")
        wself_loaded = sem("wself_loaded")
        src_loaded = sem("src_loaded")
        dst_loaded = sem("dst_loaded")
        consts = sem("consts")
        dve_step = sem("dve_step")
        zero_ready = sem("zero_ready")
        slots_zeroed = sem("slots_zeroed")
        masks = sem("masks")
        xT_made = sem("xT_made")
        xT_copied = sem("xT_copied")
        mix_ready = sem("mix_ready")
        wmix_made = sem("wmix_made")
        wmix_copied = sem("wmix_copied")
        w_stored = [sem(f"w_stored{i}") for i in range(2)]
        w_ready = [sem(f"w_ready{i}") for i in range(2)]
        xcur_ready = sem("xcur_ready")
        rows_ready = sem("rows_ready")
        word_step = sem("word_step")
        word_ready = sem("word_ready")
        digits_ready = sem("digits_ready")
        onehots_ready = sem("onehots_ready")
        ends_ready = sem("ends_ready")
        y_made = sem("y_made")
        y_copied = sem("y_copied")
        y_stored = [sem(f"y_stored{i}") for i in range(RY)]
        ranks_ready = sem("ranks_ready")
        prefix_ready = sem("prefix_ready")
        addr_ready = sem("addr_ready")
        scattered = [sem(f"scattered{i}") for i in range(2)]
        addr_copied = sem("addr_copied")
        idx_copied = sem("idx_copied")
        place_ready = sem("place_ready")
        place_used = sem("place_used")
        slots_loaded = sem("slots_loaded")
        slots_read = sem("slots_read")
        tblk_ready = sem("tblk_ready")
        gathered = [sem(f"gathered{i}") for i in range(RG)]
        rowoh_ready = sem("rowoh_ready")
        summed = sem("summed")
        act_step = sem("act_step")
        std_ready = sem("std_ready")
        normed = sem("normed")
        out_stored = sem("out_stored")

        block = ctx.enter_context(nc.Block())

        CONSTS = 7

        def edge_pieces():
            return [(0, 112), (112, 124), (124, EP)]

        @block.sync
        def _(sp):
            def load_edges(tile, a, s):
                v = a.rearrange("(p j) -> p j", p=EP)
                for lo, hi in edge_pieces():
                    sp.dma_start(tile[lo:hi, :], v[lo:hi, :]).then_inc(s, 16)

            load_edges(src_i, src, src_loaded)
            load_edges(dst_i, dst, dst_loaded)
            load_edges(type_i, etype, dst_loaded)
            sp.wait_ge(zero_ready, 1)
            sp.dma_start(slots.rearrange("(p t) o -> p (t o)", p=P), zeros[:, :]).then_inc(slots_zeroed, 16)

            rows = weights.rearrange("r (i h) o -> (r i) (h o)", h=IH)
            for half in range(2):
                sp.wait_ge(wmix_copied, 2 * (half + 1))
                sp.dma_start(rows[half * P:(half + 1) * P, :], wmix[:, half, :]).then_inc(w_stored[half], 16)
            for half in range(2):
                types = slice(half * TYPES // 2, (half + 1) * TYPES // 2)
                sp.wait_ge(w_stored[half], 16)
                sp.dma_start(W[:, types, :], weights[types, :, :].rearrange("r i o -> i r o")).then_inc(w_ready[half], 16)

            rows = table.rearrange("(n t) o -> n (t o)", t=TYPES)
            with sp.Fori(0, NFULL // RY) as g:
                for s in range(RY):
                    q = g * RY + s
                    sp.wait_ge(y_copied, YC * (q + 1))
                    sp.dma_start(rows[bass.ds(q * P, P), :], ytile[:, s, :]).then_inc(y_stored[s], 16)
            sp.wait_ge(y_copied, YC * NB)
            sp.dma_start(rows[NFULL * P:NODES, :], ytile[0:NLAST, NFULL % RY, :]).then_inc(y_stored[NFULL % RY], 16)

            for half in range(2):
                sp.wait_ge(scattered[half], 16 * SU * SCATTER_ROUNDS)
            sp.dma_start(sD[:, :], slots.rearrange("(p t) o -> p (t o)", p=P)).then_inc(slots_loaded, 16)

            rows = out[0:NFULL * P, :].rearrange("(q p) f -> p q f", p=P)
            for part in range(2):
                tiles = slice(part * NFULL // 2, (part + 1) * NFULL // 2)
                sp.wait_ge(normed, part + 1)
                sp.dma_start(rows[:, tiles, :], normal[:, tiles, :]).then_inc(out_stored, 16)
            sp.wait_ge(normed, 3)
            sp.dma_start(out[NFULL * P:NODES, :], normal[0:NLAST, NFULL, :]).then_inc(out_stored, 16)
            sp.wait_ge(out_stored, 48)

        @block.gpsimd
        def _(pool):
            nc.gpsimd.iota(own_i[:, :], [[-IC, BASES]], channel_multiplier=1).then_inc(consts, 1)
            nc.gpsimd.iota(same_i[:, :], [[-1, IC]], channel_multiplier=1).then_inc(consts, 1)
            nc.gpsimd.iota(diag[:, :], [[1, P]], channel_multiplier=-1,
                           allow_small_or_imprecise_dtypes=True).then_inc(consts, 1)
            nc.gpsimd.iota(iota_slot[:, :], [[1, P]], channel_multiplier=0,
                           allow_small_or_imprecise_dtypes=True).then_inc(consts, 1)
            nc.gpsimd.iota(iota_tile[:, :], [[1, TP]], channel_multiplier=0,
                           allow_small_or_imprecise_dtypes=True).then_inc(consts, 1)
            nc.gpsimd.iota(iota_row[:, :], [[1, BLOCK]], channel_multiplier=0,
                           allow_small_or_imprecise_dtypes=True).then_inc(consts, 1)
            nc.gpsimd.iota(iota_t1[:, :], [[1, TP]], channel_multiplier=0,
                           allow_small_or_imprecise_dtypes=True).then_inc(consts, 1)

            words = [0]

            def wstep(ins):
                words[0] += 1
                ins.then_inc(word_step, 1)
                pool.wait_ge(word_step, words[0])

            pool.wait_ge(dst_loaded, 32 * len(edge_pieces()))
            nc.gpsimd.tensor_scalar(dst_w[:, :], dst_i[:, :], float(TYPES * BLOCK), float(-SHIFT), ALU.mult, ALU.add)
            wstep(nc.gpsimd.tensor_scalar(type_w[:, :], type_i[:, :], float(BLOCK), 0.0, ALU.mult, ALU.add))
            wstep(nc.gpsimd.tensor_tensor(word0[:, :], dst_w[:, :], type_w[:, :], ALU.add))
            pool.wait_ge(rows_ready, 1)
            wstep(nc.gpsimd.tensor_copy(row_w[:, :], row_i[:, :]))
            wstep(nc.gpsimd.tensor_tensor(word1[:, :], word0[:, :], row_w[:, :], ALU.add))
            wstep(nc.gpsimd.tensor_scalar(word_pos[:, :], word1[:, :], 0.0, None, ALU.is_ge))
            nc.gpsimd.tensor_tensor(word[:, :], word1[:, :], word_pos[:, :], ALU.add).then_inc(word_ready, 1)
            pool.wait_ge(word_ready, 1)


            pool.wait_ge(slots_zeroed, 16)
            pool.wait_ge(addr_ready, 1)

            def scatter_rounds(g, first):
                for half in range(2):
                    j = (g * 2 + half) * SU + PLACED
                    if not first:
                        pool.wait_ge(scattered[half], g * (16 * SU))
                    nc.gpsimd.tensor_copy(addr_ring[:, half, :], addr_i[:, bass.ds(j, SU)]).then_inc(addr_copied, 1)
                    nc.gpsimd.tensor_copy(word_ring[:, half, :], word[:, bass.ds(j, SU)]).then_inc(addr_copied, 1)
                    pool.wait_ge(addr_copied, g * 4 + 2 * (half + 1))
                    nc.gpsimd.nop(nofuse=True)
                    for s in range(SU):
                        nc.gpsimd.indirect_dma_start(
                            out=slots[:, :],
                            out_offset=bass.IndirectOffsetOnAxis(ap=addr_ring[:, half, s:s + 1], axis=0),
                            in_=word_ring[:, half, s:s + 1], in_offset=None).then_inc(scattered[half], 16)

            scatter_rounds(0, True)
            with pool.Fori(1, SCATTER_ROUNDS) as g:
                scatter_rounds(g, False)

            def gather(half, s):
                nc.gpsimd.indirect_dma_start(
                    out=gath[:, half, s, :], out_offset=None, in_=table[:, :],
                    in_offset=bass.IndirectOffsetOnAxis(ap=idx_ring[:, half, s:s + 1], axis=0)
                ).then_inc(gathered[half * GU + s], 16)

            for s in range(RY):
                pool.wait_ge(y_stored[s], 16 * len(range(s, NB, RY)))

            def gather_round(r, half, n):
                pool.wait_ge(idx_copied, r + 1)
                nc.gpsimd.nop(nofuse=True)
                for s in range(n):
                    gather(half, s)

            gather_round(0, 0, GU)
            gather_round(1, 1, GU)
            with pool.Fori(1, TILES // RG) as g:
                for half in range(2):
                    gather_round(g * 2 + half, half, GU)
            gather_round(TILES // RG * 2, 0, TILES % RG)

        @block.scalar
        def _(act):
            act.dma_start(coef_bc[:, :, :].rearrange("p r b -> p (r b)"),
                          coefs.rearrange("r b -> (r b)").partition_broadcast(P)).then_inc(coef_loaded, 16)
            act.dma_start(bases_sb[:, :, :].rearrange("p h o -> p (h o)"),
                          bases.rearrange("b (i h) o -> (b i) (h o)", h=IH)).then_inc(bases_loaded, 16)
            act.dma_start(wself[:, :], w_self[:, :]).then_inc(wself_loaded, 16)
            act.dma_start(x_sb[:, 0:NFULL, :], x[0:NFULL * P, :].rearrange("(q p) f -> p q f", p=P)).then_inc(x_loaded, 16)
            act.wait_ge(zero_ready, 2)
            act.dma_start(x_sb[0:NLAST, NFULL, :], x[NFULL * P:NODES, :]).then_inc(x_loaded, 16)

            for half in range(2):
                for c in range(2):
                    act.wait_ge(wmix_made, 2 * half + c + 1)
                    nc.scalar.copy(wmix[:, half, c * BANK:(c + 1) * BANK], ps[:, 2 * half + c, :]).then_inc(wmix_copied, 1)

            def next_x(q, s):
                nc.scalar.copy(xcur[:, s, :], xT[:, bass.ds(q, 1), :].rearrange("p o n -> p (o n)")).then_inc(xcur_ready, 1)

            for g in range(XG):
                n = min(4, NB - 4 * g)
                act.wait_ge(xT_made, g + 1)
                nc.scalar.copy(xT[:, 4 * g:4 * g + n, :].rearrange("p q n -> p (q n)"),
                               ps[:, 4 + g % 4, 0:n * P]).then_inc(xT_copied, 1)
                if g == 0:
                    act.wait_ge(xT_copied, 1)
                    next_x(0, 0)
                    next_x(1, 1)
            nc.scalar.copy(wselfT[:, :], ps[:, 4 + (XG - 1) % 4, P:2 * P]).then_inc(xT_copied, 1)

            def copy_bank(q, s, c):
                act.wait_ge(y_made, YC * q + c + 1)
                nc.scalar.copy(ytile[:, s, c * BANK:(c + 1) * BANK], ps[:, c, :]).then_inc(y_copied, 1)

            def digits(n, c, count=PC):
                for v in range(c * PC, c * PC + count):
                    if v in ACT_DIGITS:
                        j = n * RP + v
                        act.wait_ge(onehots_ready, j + 1)
                        for d, digit in enumerate((hi_f, lo_f)):
                            last = nc.scalar.activation(slotoh[:, v, d, :], oneslot[:, v, :], ACT.Copy,
                                                        scale=digit[:, bass.ds(j, 1)])
                        last.then_inc(place_ready, 1)

            def copy_tile(q, s, group=None, ahead=True):
                for c in range(YC):
                    if group is not None:
                        digits(group + (c + 1) // YC, (c + 1) % YC)
                    copy_bank(q, s, c)
                if ahead:
                    next_x(q + 2, s % 2)

            act.wait_ge(xT_copied, XG + 1)
            for q in range(EARLY):
                if q >= RY:
                    act.wait_ge(y_stored[q % RY], 16 * (q // RY))
                copy_tile(q, q % RY)
            act.wait_ge(digits_ready, 1)
            digits(0, 0)
            with act.Fori(0, GROUPS // RY) as g:
                for u in range(RY):
                    q, s = g * RY + EARLY + u, (EARLY + u) % RY
                    act.wait_ge(y_stored[s], g * 16 + 16 * ((EARLY + u) // RY))
                    copy_tile(q, s, group=g * RY + u)
            for q in range(EARLY + GROUPS // RY * RY, NB):
                act.wait_ge(y_stored[q % RY], 16 * (q // RY))
                copy_tile(q, q % RY, group=q - EARLY, ahead=q + 2 < NB)
            for c in range(1, -(-TRAIL // PC)):
                digits(GROUPS, c, min(PC, TRAIL - c * PC))

            steps = [0]

            def step(ins):
                steps[0] += 1
                ins.then_inc(act_step, 1)
                act.wait_ge(act_step, steps[0])

            act.wait_ge(ends_ready, 1)
            for y in y_stored:
                act.wait_ge(y, 16 * (NB // RY))
            for b in range(-(-NB // 4)):
                n = min(4, NB - 4 * b)
                if b < BLOCKS // 2:
                    done = act.value_load(ends_i[0:1, 2 * b + 1:2 * b + 2], min_val=1, max_val=TILES)
                    act.wait_ge(summed, done)
                else:
                    act.wait_ge(summed, TILES)
                for q in range(4 * b, 4 * b + n):
                    last = nc.scalar.activation(h[:, q, :], acc[:, q * D:(q + 1) * D], ACT.Copy, accum_out=hsum[:, q:q + 1])
                step(last)
                step(nc.scalar.mul(hneg[:, 4 * b:4 * b + n], hsum[:, 4 * b:4 * b + n], -1.0 / D))
                for q in range(4 * b, 4 * b + n):
                    last = nc.scalar.activation(sq[:, q % 4, :], h[:, q, :], ACT.Square, bias=hneg[:, q:q + 1],
                                                accum_out=hvar[:, q:q + 1])
                step(last)
                nc.scalar.activation(hstd[:, 4 * b:4 * b + n], hvar[:, 4 * b:4 * b + n], ACT.Sqrt, bias=eps_c[:, 0:1],
                                     scale=1.0 / D).then_inc(std_ready, 1)

        @block.vector
        def _(dve):
            steps = [0]

            def step(ins):
                steps[0] += 1
                ins.then_inc(dve_step, 1)
                dve.wait_ge(dve_step, steps[0])

            nc.vector.memset(zeros[:, :], 0.0).then_inc(zero_ready, 1)
            nc.vector.memset(x_sb[:, NFULL, :], 0.0).then_inc(zero_ready, 1)
            nc.vector.memset(zeros_h[:, :], 0.0).then_inc(zero_ready, 1)
            nc.vector.memset(ones_row[:, :], 1.0)
            nc.vector.memset(eps_c[:, :], EPS)
            nc.vector.memset(ones[:, :], 1.0).then_inc(masks, 1)
            dve.wait_ge(consts, CONSTS)
            nc.vector.tensor_scalar(ident[:, :], diag[:, :], 0.0, None, ALU.is_equal).then_inc(masks, 1)
            nc.vector.tensor_scalar(before[:, :], diag[:, :], 0.0, None, ALU.is_gt).then_inc(masks, 1)
            dve.wait_ge(masks, 3)

            nc.vector.tensor_scalar(own_s[:, :], own_i[:, :], IC.bit_length() - 1, None, ALU.arith_shift_right)
            step(nc.vector.tensor_scalar(same_m[:, :], same_i[:, :], IC - 1, None, ALU.bitwise_and))
            nc.vector.tensor_scalar(own[:, :], own_s[:, :], 0.0, None, ALU.is_equal)
            step(nc.vector.tensor_scalar(same[:, :], same_m[:, :], 0.0, None, ALU.is_equal))
            dve.wait_ge(coef_loaded, 16)
            step(nc.vector.tensor_tensor(coef_own[:, :, :], coef_bc[:, :, :], own[:, :].unsqueeze(1).broadcast_to([P, TYPES, BASES]),
                                         ALU.mult))
            step(nc.vector.tensor_reduce(coef_col[:, :], coef_own[:, :, :], AX_X, ALU.add))
            nc.vector.tensor_tensor(mix[:, :, :], coef_col[:, :].unsqueeze(2).broadcast_to([P, TYPES, IC]),
                                    same[:, :].unsqueeze(1).broadcast_to([P, TYPES, IC]), ALU.mult).then_inc(mix_ready, 1)

            dve.wait_ge(src_loaded, 16 * len(edge_pieces()))
            nc.vector.tensor_scalar(row_i[:, :], src_i[:, :], BLOCK - 1, None, ALU.bitwise_and).then_inc(rows_ready, 1)
            step(nc.vector.tensor_scalar(blk_i[:, :], src_i[:, :], BLOCK.bit_length() - 1, None, ALU.arith_shift_right))
            step(nc.vector.tensor_copy(blk_h[:, :], blk_i[:, :]))
            for k in range(BLOCKS):
                last = nc.vector.tensor_scalar(inblk[:, k, :], blk_h[:, :], float(k), None, ALU.is_equal)
            step(last)
            for k in range(BLOCKS):
                last = nc.vector.tensor_tensor_scan(rank[:, k, :], ones_row[0:EP, :], inblk[:, k, :], 0.0, ALU.mult, ALU.add)
            last.then_inc(ranks_ready, 1)

            dve.wait_ge(prefix_ready, 1)
            step(nc.vector.tensor_scalar(need_i[:, :], ps_total, float(P - 1), None, ALU.add))
            step(nc.vector.tensor_scalar(need_t[:, :], need_i[:, :], P.bit_length() - 1, None, ALU.arith_shift_right))
            step(nc.vector.tensor_copy(need_f[:, :], need_t[:, :]))
            step(nc.vector.tensor_tensor_scan(ends[:, :], ones_row[:, 0:BLOCKS], need_f[:, :], 0.0, ALU.mult, ALU.add))
            step(nc.vector.tensor_tensor(starts[:, :], ends[:, :], need_f[:, :], ALU.subtract))
            step(nc.vector.scalar_tensor_tensor(offs[:, :], starts[0:EP, :], float(P), ps_before, ALU.mult, ALU.add))
            def sorted_slots(lo, hi):
                for k in range(BLOCKS):
                    last = nc.vector.scalar_tensor_tensor(rank[:, k, lo:hi], rank[:, k, lo:hi], offs[:, k:k + 1],
                                                          inblk[:, k, lo:hi], ALU.add, ALU.mult)
                step(last)
                step(nc.vector.tensor_reduce(pos_f[:, lo:hi], rank[:, :, lo:hi].rearrange("p k j -> p j k"), AX_X, ALU.add))
                step(nc.vector.tensor_scalar(pos_i[:, lo:hi], pos_f[:, lo:hi], -1.0, None, ALU.add))
                nc.vector.tensor_scalar(tile_i[:, lo:hi], pos_i[:, lo:hi], P.bit_length() - 1, None, ALU.arith_shift_right)
                step(nc.vector.tensor_scalar(slot_i[:, lo:hi], pos_i[:, lo:hi], P - 1, None, ALU.bitwise_and))

            sorted_slots(PLACED, EJ)
            nc.vector.scalar_tensor_tensor(addr_i[:, PLACED:], slot_i[:, PLACED:], float(TP), tile_i[:, PLACED:],
                                           ALU.mult, ALU.add).then_inc(addr_ready, 1)
            sorted_slots(0, PLACED)
            nc.vector.tensor_copy(tile_f[:, 0:PLACED], tile_i[:, 0:PLACED])
            step(nc.vector.tensor_copy(slot_f[:, 0:PLACED], slot_i[:, 0:PLACED]))

            dve.wait_ge(word_ready, 1)
            step(nc.vector.tensor_scalar(wdig_i[:, :], word[:, :], float(DIGIT // 2), None, ALU.add))
            nc.vector.tensor_scalar(hi_i[:, :], wdig_i[:, :], DIGIT.bit_length() - 1, None, ALU.arith_shift_right)
            step(nc.vector.tensor_scalar(lo_i[:, :], wdig_i[:, :], DIGIT - 1, None, ALU.bitwise_and))
            nc.vector.tensor_copy(hi_f[:, :], hi_i[:, :])
            nc.vector.tensor_scalar(lo_f[:, :], lo_i[:, :], float(-DIGIT // 2), None, ALU.add).then_inc(digits_ready, 1)
            dve.wait_ge(digits_ready, 1)

            step(nc.vector.tensor_scalar(tblk_a[:, :], iota_t1[:, :], ends[0:1, 0:1], None, ALU.is_ge))
            now, other = tblk_a, tblk_b
            for k in range(1, BLOCKS - 1):
                step(nc.vector.scalar_tensor_tensor(other[:, :], iota_t1[:, :], ends[0:1, k:k + 1], now[:, :], ALU.is_ge, ALU.add))
                now, other = other, now
            nc.vector.tensor_scalar(tblk_i[:, :], now[:, :], float(BLOCK), None, ALU.mult).then_inc(tblk_ready, 1)
            nc.vector.tensor_scalar(ends_i[:, :], ends[0:1, :], 1.0, None, ALU.max).then_inc(ends_ready, 1)

            def place(j, s):
                slot = slot_f[:, bass.ds(j, 1)]
                if s in DVE_DIGITS:
                    for d, digit in enumerate((hi_f, lo_f)):
                        nc.vector.tensor_scalar(slotoh[:, s, d, :], iota_slot[0:EP, :], slot, digit[:, bass.ds(j, 1)],
                                                ALU.is_equal, ALU.mult)
                else:
                    nc.vector.tensor_scalar(oneslot[:, s, :], iota_slot[0:EP, :], slot, None, ALU.is_equal)
                nc.vector.tensor_scalar(tileoh[:, s, :], iota_tile[0:EP, :], tile_f[:, bass.ds(j, 1)], None,
                                        ALU.is_equal).then_inc(onehots_ready, 1)

            for j in range(RP):
                place(j, j)
            with dve.Fori(1, PLACED // RP) as g:
                for s in range(RP):
                    j = g * RP + s
                    dve.wait_ge(place_used, j - (RP - 1))
                    place(j, s)
            for j in range(PLACED // RP * RP, PLACED):
                dve.wait_ge(place_used, j - (RP - 1))
                place(j, j % RP)
            dve.wait_ge(place_used, PLACED)
            dve.wait_ge(slots_loaded, 16)
            reads = [0]

            def table_rows(lo, hi):
                step(nc.vector.scalar_tensor_tensor(sw0[:, lo:hi], ps_hi[:, lo:hi], float(DIGIT), sD[:, lo:hi], ALU.mult, ALU.add))
                nc.vector.tensor_tensor(sw[:, lo:hi], ps_lo[:, lo:hi], sw0[:, lo:hi], ALU.add).then_inc(slots_read, 1)
                reads[0] += 1
                dve.wait_ge(slots_read, reads[0])
                step(nc.vector.scalar_tensor_tensor(sneg[:, lo:hi], sw[:, lo:hi], 0.0, sw[:, lo:hi], ALU.is_gt, ALU.subtract))
                step(nc.vector.tensor_scalar(sval[:, lo:hi], sneg[:, lo:hi], -1.0, float(SHIFT), ALU.mult, ALU.add))
                step(nc.vector.tensor_scalar(sidx[:, lo:hi], sval[:, lo:hi], BLOCK.bit_length() - 1, None, ALU.arith_shift_right))

            table_rows(0, RG)
            for half in range(2):
                nc.vector.tensor_copy(idx_ring[:, half, :], sidx[:, half * GU:(half + 1) * GU]).then_inc(idx_copied, 1)
            table_rows(RG, TP)
            nc.vector.tensor_scalar(sempty[:, :], sw[:, :], 0.0, float(2 * BLOCK), ALU.is_equal, ALU.mult)
            step(nc.vector.tensor_scalar(srow_i[:, :], sval[:, :], BLOCK - 1, None, ALU.bitwise_and))
            step(nc.vector.tensor_tensor(srow[:, :], srow_i[:, :], sempty[:, :], ALU.add))

            def copy_indices(r, half, n):
                nc.vector.tensor_copy(idx_ring[:, half, 0:n], sidx[:, bass.ds(r * GU, n)]).then_inc(idx_copied, 1)

            def row_onehot(t, s):
                nc.vector.tensor_scalar(rowoh[:, s, :], iota_row[:, :], srow[:, bass.ds(t, 1)], None,
                                        ALU.is_equal).then_inc(rowoh_ready, 1)

            for t in range(RG):
                row_onehot(t, t)
            with dve.Fori(1, TILES // RG) as g:
                for half in range(2):
                    r = g * 2 + half
                    dve.wait_ge(summed, r * GU - GU)
                    copy_indices(r, half, GU)
                    for s in range(GU):
                        row_onehot(r * GU + s, half * GU + s)
            dve.wait_ge(summed, (TILES // GU - 1) * GU)
            copy_indices(TILES // GU, 0, TILES % GU)
            for t in range(TILES // RG * RG, TILES):
                row_onehot(t, t % RG)

            def normalise(first, end, banks, parts):
                dve.wait_ge(std_ready, banks)
                step(nc.vector.reciprocal(hinv[:, first:end], hstd[:, first:end]))
                for q in range(first, end):
                    last = nc.vector.tensor_scalar(normal[:, q, :], h[:, q, :], hneg[:, q:q + 1], hinv[:, q:q + 1],
                                                   ALU.add, ALU.mult)
                    if (q + 1 - first) % ((end - first) // parts) == 0:
                        last.then_inc(normed, 1)

            normalise(0, NFULL, NFULL // 4, 2)
            normalise(NFULL, NB, NFULL // 4 + 1, 1)

        @block.tensor
        def _(pe):
            def keep_warm(n):
                for _ in range(n):
                    nc.tensor.matmul(ps[:, 7, 0:TP], zeros_h[:, 0:P], zeros_h[:, :], start=True, stop=True)

            pe.wait_ge(zero_ready, 3)
            keep_warm(WARM[0])

            pe.wait_ge(mix_ready, 1)
            pe.wait_ge(bases_loaded, 16)
            for half in range(2):
                for c in range(2):
                    nc.tensor.matmul(ps[:, 2 * half + c, :],
                                     mix[:, half * TYPES // 2:(half + 1) * TYPES // 2, :].rearrange("p r i -> p (r i)"),
                                     bases_sb[:, c * IH // 2:(c + 1) * IH // 2, :].rearrange("p h o -> p (h o)"),
                                     start=True, stop=True).then_inc(wmix_made, 1)

            pe.wait_ge(masks, 3)
            pe.wait_ge(x_loaded, 32)
            for g in range(XG):
                n = min(4, NB - 4 * g)
                if g >= 4:
                    pe.wait_ge(xT_copied, g - 3)
                for i in range(n):
                    last = nc.tensor.transpose(ps[:, 4 + g % 4, i * P:(i + 1) * P], x_sb[:, 4 * g + i, :], ident[:, :])
                if g == XG - 1:
                    pe.wait_ge(wself_loaded, 16)
                    last = nc.tensor.transpose(ps[:, 4 + g % 4, P:2 * P], wself[:, :], ident[:, :])
                last.then_inc(xT_made, 1)

            def prefix():
                pe.wait_ge(ranks_ready, 1)
                nc.tensor.matmul(ps_before, before[0:EP, 0:EP], rank[:, :, EJ - 1], start=True, stop=True)
                nc.tensor.matmul(ps_total, ones[0:EP, :], rank[:, :, EJ - 1], start=True, stop=True).then_inc(prefix_ready, 1)

            def table_bank(q, s, c, first=False):
                if first and c % 2 == 0:
                    pe.wait_ge(w_ready[c // 2], 16)
                if not first:
                    pe.wait_ge(y_copied, YC * q + c - (YC - 1))
                nc.tensor.matmul(ps[:, c, :], xcur[:, s, :], W[:, c * 4:(c + 1) * 4, :].rearrange("p r o -> p (r o)"),
                                 start=True, stop=True).then_inc(y_made, 1)

            def table_tile(q, s):
                pe.wait_ge(xcur_ready, q + 1)
                for c in range(YC):
                    table_bank(q, s, c)

            pe.wait_ge(xT_copied, 4)
            keep_warm(WARM[1])
            prefix()
            pe.wait_ge(xcur_ready, 1)
            pe.wait_ge(wmix_copied, 4)
            for c in range(YC):
                table_bank(0, 0, c, first=True)
            with pe.Fori(0, (EARLY - 1) // 2) as g:
                table_tile(g * 2 + 1, 1)
                table_tile(g * 2 + 2, 0)
            for q in range(1 + (EARLY - 1) // 2 * 2, EARLY):
                table_tile(q, q % 2)

            pe.wait_ge(xT_copied, XG + 1)
            for ps_digit in (ps_hi, ps_lo):
                nc.tensor.matmul(ps_digit, zeros_h[:, 0:P], zeros_h[:, :], start=True, stop=False, skip_group_check=True)

            def place(n, s):
                j = n * RP + s
                if s in DVE_DIGITS:
                    pe.wait_ge(onehots_ready, j + 1)
                else:
                    pe.wait_ge(place_ready, n * len(ACT_DIGITS) + ACT_DIGITS.index(s) + 1)
                nc.tensor.matmul(ps_hi, slotoh[:, s, 0, :], tileoh[:, s, :], start=False, stop=False, skip_group_check=True)
                nc.tensor.matmul(ps_lo, slotoh[:, s, 1, :], tileoh[:, s, :], start=False, stop=False,
                                 skip_group_check=True).then_inc(place_used, 1)

            def table_tile_and_group(q, s, n):
                pe.wait_ge(xcur_ready, q + 1)
                for c in range(YC):
                    table_bank(q, s, c)
                    for v in range(c * PC, (c + 1) * PC):
                        place(n, v)

            with pe.Fori(0, GROUPS // 2) as g:
                for u in range(2):
                    table_tile_and_group(g * 2 + EARLY + u, (EARLY + u) % 2, g * 2 + u)
            for n in range(GROUPS // 2 * 2, GROUPS):
                table_tile_and_group(EARLY + n, (EARLY + n) % 2, n)
            for v in range(TRAIL):
                place(GROUPS, v)

            pe.wait_ge(y_copied, YC * NB)
            hold_words = [q for q in range(NB) if q // 4 in (4, 5)]
            for q in [q for q in range(NB) if q not in hold_words] + hold_words:
                if q == hold_words[0]:
                    pe.wait_ge(slots_read, 2)
                nc.tensor.matmul(acc[:, q * P:(q + 1) * P], xT[:, q, :], wselfT[:, :], start=(q % 4 == 0), stop=False,
                                 skip_group_check=True)
                nc.tensor.matmul(acc[:, q * P:(q + 1) * P], xT[:, q, :], ident[:, :], start=False, stop=False,
                                 skip_group_check=True)

            def block_columns(t, n):
                _, cols = nc.values_load_multi_w_load_instructions(
                    tblk_i[0:1, bass.ds(t, n)], engines=[mybir.EngineType.PE], min_val=0, max_val=(BLOCKS - 1) * BLOCK,
                    skip_runtime_bounds_check_because="it is a count of up to BLOCKS - 1 blocks times BLOCK")
                return cols

            def add_tile(g, s, col):
                t = g * RG + s
                pe.wait_ge(rowoh_ready, t + 1)
                pe.wait_ge(gathered[s], 16 * (g + 1))
                for c in range(BLOCK // P):
                    last = nc.tensor.matmul(acc[:, bass.ds(col + c * P, P)], rowoh[:, s, c * P:(c + 1) * P],
                                            gath[:, s // GU, s % GU, :], start=False, stop=False, skip_group_check=True)
                last.then_inc(summed, 1)

            pe.wait_ge(tblk_ready, 1)
            with pe.Fori(0, TILES // RG) as g:
                for s0 in range(0, RG, GU):
                    for i, col in enumerate(block_columns(g * RG + s0, GU)):
                        add_tile(g, s0 + i, col)
            for s, col in enumerate(block_columns(TILES // RG * RG, TILES % RG)):
                add_tile(TILES // RG, s, col)


def kernel(x, src, dst, edge_type_16, L0_gnn_bases, L0_gnn_coefficients, L0_gnn_w_self):
    import numpy as np
    import concourse.bacc as bacc
    from concourse.bass_utils import run_bass_kernel_spmd

    nc = bacc.Bacc("TRN2", target_bir_lowering=False, num_devices=1)
    named = dict(x=x, src=src, dst=dst, etype=edge_type_16, bases=L0_gnn_bases, coefs=L0_gnn_coefficients,
                 w_self=L0_gnn_w_self)
    arrays, args = {}, []
    for name, a in named.items():
        a = np.ascontiguousarray(a)
        arrays[f"in_{name}"] = a
        args.append(nc.dram_tensor(f"in_{name}", a.shape, mybir.dt.from_np(a.dtype), kind="ExternalInput").ap())
    out = nc.dram_tensor("out_0", (NODES, D), F32, kind="ExternalOutput").ap()
    rgcn(nc, *args, out)
    r = run_bass_kernel_spmd(nc, [arrays], core_ids=[0])
    return r.results[0]["out_0"]
```

```python
from contextlib import ExitStack

import concourse.bass as bass
from concourse import mybir

F32 = mybir.dt.float32
F32R = mybir.dt.float32r
F16 = mybir.dt.float16
BF16 = mybir.dt.bfloat16
I32 = mybir.dt.int32
ALU = mybir.AluOpType
ACT = mybir.ActivationFunctionType
AX_X = mybir.AxisListType.X

P = 128
NODES = 3125
D = 128
TYPES = 16
BASES = 8
EDGES = 50000
EPS = 1e-5

NB = -(-NODES // P)
XG = -(-NB // 4)
WARM = (12, 10)
NFULL = NODES // P
NLAST = NODES - NFULL * P
BLOCK = 256
BLOCKS = -(-NODES // BLOCK)
EP = 125
EJ = EDGES // EP
SPLIT = 151
EMPTY = BLOCKS * (P - 1)
TA = (SPLIT * EP + EMPTY) // P
TB = ((EJ - SPLIT) * EP + EMPTY) // P
TILES = TA + TB
BANK = 512
YCOLS = TYPES * D
YC = YCOLS // BANK

SHIFT = NODES * TYPES * BLOCK // 2
DIGIT = 4096

RY = 4
RP = 16
BEFORE_PREFIX = 5
EARLY = 10
GROUPS = NB - EARLY
TRAIL = 19
PLACED = GROUPS * YC + TRAIL
SU = 12
SCATTER_ROUNDS = (SPLIT - PLACED) // (2 * SU)
assert SCATTER_ROUNDS * 2 * SU == SPLIT - PLACED
GU = 8
RG = 2 * GU
PB = 14
PLACE_PAIRS = -(-(EJ - SPLIT) // (2 * PB))
SELF_PAIRS = 2
EJB = SPLIT + PLACE_PAIRS * 2 * PB
DVE_DIGITS = (4, 11)
ACT_DIGITS = [v for v in range(PB) if v not in DVE_DIGITS]
assert RP == RY * YC and NFULL % (PLACE_PAIRS - 1) == 0
assert TA % RG == 0 and TB % RG == 0 and 2 * TB <= BANK and PLACE_PAIRS < TA // RG < PLACE_PAIRS + SELF_PAIRS
IC = P // BASES
IH = D // IC


def rgcn(nc, x, src, dst, etype, bases, coefs, w_self, out):
    ctx = ExitStack()
    with ctx:
        def sb(name, shape, dt):
            return ctx.enter_context(nc.sbuf_tensor(name, shape, dt))

        def sem(name):
            return ctx.enter_context(nc.semaphore(name))

        weights = nc.dram_tensor("weights", (TYPES, D, D), F32).ap()
        table = nc.dram_tensor("table", (NODES * TYPES, D), F32).ap()
        slots = nc.dram_tensor("slots", (P * TA, 1), F32).ap()

        x_sb = sb("x_sb", [P, NB, D], F32)
        xT = sb("xT", [P, 2, NB, P], F32R)
        bases_sb = sb("bases_sb", [P, IH, D], F32)
        coef_bc = sb("coef_bc", [P, TYPES, BASES], F32)
        own_i = sb("own_i", [P, BASES], I32)
        own_s = sb("own_s", [P, BASES], I32)
        own = sb("own", [P, BASES], F32)
        same_i = sb("same_i", [P, IC], I32)
        same_m = sb("same_m", [P, IC], I32)
        same = sb("same", [P, IC], F32)
        coef_own = sb("coef_own", [P, TYPES, BASES], F32)
        coef_col = sb("coef_col", [P, TYPES], F32)
        mix = sb("mix", [P, TYPES, IC], F32)
        xT_whole = sb("xT_whole", [P, NB, P], F32)
        xcur = sb("xcur", [P, 2, 2, P], F32R)
        wself = sb("wself", [P, D], F32)
        wselfT = sb("wselfT", [P, D], F32)
        W_high = sb("W_high", [P, YCOLS], F32R)
        W_low = sb("W_low", [P, YCOLS], F32R)
        ytile = sb("ytile", [P, RY, YCOLS], F32)
        wmix = ytile[:, RY - 1, :].rearrange("p (a c) -> p a c", a=2)
        W = ytile[:, RY - 2, :]

        diag = sb("diag", [P, P], F32)
        ident = sb("ident", [P, P], F32)
        before = sb("before", [P, P], F32)
        ones = sb("ones", [P, P], F32)
        ones_row = sb("ones_row", [P, EJ], F32)
        zeros = sb("zeros", [P, TA], F32)
        iota_slot = sb("iota_slot", [P, P], F16)
        iota_tile = sb("iota_tile", [P, TB], F16)
        iota_row = sb("iota_row", [P, BLOCK], F32)
        iota_t1 = sb("iota_t1", [1, TB], F32)

        src_i = sb("src_i", [EP, EJ], I32)
        dst_i = sb("dst_i", [EP, EJ], I32)
        type_i = sb("type_i", [EP, EJ], I32)
        blk_i = sb("blk_i", [EP, EJ], I32)
        blk_h = sb("blk_h", [EP, EJ], BF16)
        row_i = sb("row_i", [EP, EJ], I32)
        inblk = sb("inblk", [EP, BLOCKS, EJ], BF16)
        rank_all = sb("rank", [P, BLOCKS, EJ], F32)
        rank = rank_all[0:EP, :, :]
        offs = sb("offs", [EP, 2, BLOCKS], F32)
        need_i = sb("need_i", [P, 2, BLOCKS], I32)
        need_t = sb("need_t", [P, 2, BLOCKS], I32)
        need_f = sb("need_f", [P, 2, BLOCKS], F32)
        ends = sb("ends", [P, 2, BLOCKS], F32)
        starts = sb("starts", [P, 2, BLOCKS], F32)
        pos_f = sb("pos_f", [EP, EJ], F32)
        pos_i = blk_i
        tile_i = sb("tile_i", [EP, EJ], I32)
        slot_i = sb("slot_i", [EP, EJ], I32)
        tile_f = sb("tile_f", [EP, EJB], F32)
        slot_f = sb("slot_f", [EP, EJB], F32)
        addr_i = sb("addr_i", [EP, EJ], I32)
        word = sb("word", [EP, EJ], F32)
        hi_f = sb("hi_f", [EP, EJB], F32)
        lo_f = sb("lo_f", [EP, EJB], F32)
        tblk = [sb(f"tblk{i}", [1, TB], F32) for i in range(2)]
        tblk_i = sb("tblk_i", [1, TILES], I32)
        ends_i = sb("ends_i", [1, BLOCKS], I32)
        dst_w = sb("dst_w", [EP, EJ], F32)
        type_w = sb("type_w", [EP, EJ], F32)
        row_w = sb("row_w", [EP, EJ], F32)

        word0, word1, word_pos = type_w, row_w, dst_w
        wdig_i, hi_i, lo_i = dst_i, type_i, row_i

        zeros_h = sb("zeros_h", [P, BANK], F16)
        oneslot = sb("oneslot", [EP, PB, P], F16)
        slotoh = sb("slotoh", [EP, RP, 2, P], F16)
        tileoh = sb("tileoh", [EP, RP, TB], F16)

        sD = sb("sD", [P, TA], F32)
        sw0, sw = [bases_sb[:, :, :].rearrange("p h o -> p (h o)")[:, i * BANK:i * BANK + TILES] for i in range(2)]
        sval = sb("sval", [P, TILES], I32)
        sidx = sb("sidx", [P, TILES], I32)
        srow_i = sb("srow_i", [P, TILES], I32)
        srow = sb("srow", [P, TILES], F32)
        sneg = sempty = sw0

        idx_ring = sb("idx_ring", [P, 2, GU], I32)
        addr_ring = sb("addr_ring", [EP, 2, SU], I32)
        word_ring = sb("word_ring", [EP, 2, SU], F32)
        rowoh = rank_all[:, :, :].rearrange("p k j -> p (k j)")[:, 0:RG * BLOCK].rearrange("p (t r) -> p t r", t=RG)

        gath = x_sb[:, 0:RG, :].rearrange("p (h s) f -> p h s f", h=2)

        in_ytile = ytile[:, :, :].rearrange("p s c -> p (s c)")
        h = in_ytile[:, 0:NB * D].rearrange("p (q f) -> p q f", q=NB)
        normal = in_ytile[:, NB * D:2 * NB * D].rearrange("p (q f) -> p q f", q=NB)
        sq = xT_whole[:, 0:4, :]
        hsum = sb("hsum", [P, NB], F32)
        hneg = sb("hneg", [P, NB], F32)
        hvar = sb("hvar", [P, NB], F32)
        hstd = sb("hstd", [P, NB], F32)
        hinv = sb("hinv", [P, NB], F32)
        eps_c = sb("eps_c", [P, 1], F32)

        ps = ctx.enter_context(nc.psum_tensor("ps", [P, 8, BANK], F32))
        acc = ps[:, 0:7, :].rearrange("p b c -> p (b c)")
        ps_digits = [[ps[:, bank, d * TB:d * TB + n] for d in range(2)] for bank, n in ((4, TA), (7, TB))]
        ps_before = [ps[0:EP, 7, part * 2 * BLOCKS:(part * 2 + 1) * BLOCKS] for part in range(2)]
        ps_total = [ps[:, 7, (part * 2 + 1) * BLOCKS:(part * 2 + 2) * BLOCKS] for part in range(2)]

        x_loaded = sem("x_loaded")
        bases_loaded = sem("bases_loaded")
        coef_loaded = sem("coef_loaded")
        wself_loaded = sem("wself_loaded")
        src_loaded = sem("src_loaded")
        dst_loaded = sem("dst_loaded")
        consts = sem("consts")
        dve_step = sem("dve_step")
        zero_ready = sem("zero_ready")
        slots_zeroed = sem("slots_zeroed")
        masks = sem("masks")
        xT_made = sem("xT_made")
        xT_copied = sem("xT_copied")
        mix_ready = sem("mix_ready")
        wmix_made = sem("wmix_made")
        wmix_copied = sem("wmix_copied")
        w_stored = [sem(f"w_stored{i}") for i in range(2)]
        w_ready = [sem(f"w_ready{i}") for i in range(2)]
        x_low = sem("x_low")
        x_whole = sem("x_whole")
        self_added = sem("self_added")
        w_high = sem("w_high")
        w_low = sem("w_low")
        xcur_ready = sem("xcur_ready")
        rows_ready = sem("rows_ready")
        word_step = sem("word_step")
        word_ready = sem("word_ready")
        digits_ready = sem("digits_ready")
        onehots_ready = [sem(f"onehots_ready{i}") for i in range(2)]
        ends_ready = sem("ends_ready")
        tblk_ready = sem("tblk_ready")
        y_made = sem("y_made")
        y_copied = sem("y_copied")
        y_stored = [sem(f"y_stored{i}") for i in range(RY)]
        ranks_ready = sem("ranks_ready")
        prefix_ready = sem("prefix_ready")
        addr_ready = sem("addr_ready")
        scattered = [sem(f"scattered{i}") for i in range(2)]
        addr_copied = sem("addr_copied")
        idx_copied = sem("idx_copied")
        place_digits = [sem(f"place_digits{i}") for i in range(2)]
        place_used = [sem(f"place_used{i}") for i in range(2)]
        slots_loaded = sem("slots_loaded")
        slots_read = sem("slots_read")
        gathered = [sem(f"gathered{i}") for i in range(RG)]
        rowoh_ready = sem("rowoh_ready")
        summed = sem("summed")
        act_step = sem("act_step")
        std_ready = sem("std_ready")
        normed = sem("normed")
        out_stored = sem("out_stored")

        block = ctx.enter_context(nc.Block())

        CONSTS = 7

        def edge_pieces():
            return [(0, 112), (112, 124), (124, EP)]

        def share(i):
            return range(i * PB // GU, (i + 1) * PB // GU)

        def load_edges(engine, tile, a, s):
            v = a.rearrange("(p j) -> p j", p=EP)
            for lo, hi in edge_pieces():
                engine.dma_start(tile[lo:hi, :], v[lo:hi, :]).then_inc(s, 16)

        @block.sync
        def _(sp):
            load_edges(sp, src_i, src, src_loaded)
            load_edges(sp, dst_i, dst, dst_loaded)
            sp.wait_ge(zero_ready, 1)
            sp.dma_start(slots.rearrange("(p t) o -> p (t o)", p=P), zeros[:, :]).then_inc(slots_zeroed, 16)

            rows = weights.rearrange("r (i h) o -> (r i) (h o)", h=IH)
            for half in range(2):
                sp.wait_ge(wmix_copied, 2 * (half + 1))
                sp.dma_start(rows[half * P:(half + 1) * P, :], wmix[:, half, :]).then_inc(w_stored[half], 16)
            for half in range(2):
                types = slice(half * TYPES // 2, (half + 1) * TYPES // 2)
                sp.wait_ge(w_stored[half], 16)
                sp.dma_start(W.rearrange("p (r o) -> p r o", r=TYPES)[:, types, :], weights[types, :, :].rearrange("r i o -> i r o")).then_inc(w_ready[half], 16)

            rows = table.rearrange("(n t) o -> n (t o)", t=TYPES)
            with sp.Fori(0, NFULL // RY) as g:
                for s in range(RY):
                    q = g * RY + s
                    sp.wait_ge(y_copied, YC * (q + 1))
                    sp.dma_start(rows[bass.ds(q * P, P), :], ytile[:, s, :]).then_inc(y_stored[s], 16)
            for half in range(2):
                sp.wait_ge(scattered[half], 16 * SU * SCATTER_ROUNDS)
            sp.dma_start(sD[:, :], slots.rearrange("(p t) o -> p (t o)", p=P)).then_inc(slots_loaded, 16)


            rows = out[0:NFULL * P, :].rearrange("(q p) f -> p q f", p=P)
            for part in range(2):
                tiles = slice(part * NFULL // 2, (part + 1) * NFULL // 2)
                sp.wait_ge(normed, part + 1)
                sp.dma_start(rows[:, tiles, :], normal[:, tiles, :]).then_inc(out_stored, 16)
            sp.wait_ge(normed, 3)
            sp.dma_start(out[NFULL * P:NODES, :], normal[0:NLAST, NFULL, :]).then_inc(out_stored, 16)
            sp.wait_ge(out_stored, 48)

        @block.gpsimd
        def _(pool):
            nc.gpsimd.iota(own_i[:, :], [[-IC, BASES]], channel_multiplier=1).then_inc(consts, 1)
            nc.gpsimd.iota(same_i[:, :], [[-1, IC]], channel_multiplier=1).then_inc(consts, 1)
            nc.gpsimd.iota(diag[:, :], [[1, P]], channel_multiplier=-1,
                           allow_small_or_imprecise_dtypes=True).then_inc(consts, 1)
            nc.gpsimd.iota(iota_slot[:, :], [[1, P]], channel_multiplier=0,
                           allow_small_or_imprecise_dtypes=True).then_inc(consts, 1)
            nc.gpsimd.iota(iota_tile[:, :], [[1, TB]], channel_multiplier=0,
                           allow_small_or_imprecise_dtypes=True).then_inc(consts, 1)
            nc.gpsimd.iota(iota_row[:, :], [[1, BLOCK]], channel_multiplier=0,
                           allow_small_or_imprecise_dtypes=True).then_inc(consts, 1)
            nc.gpsimd.iota(iota_t1[:, :], [[1, TB]], channel_multiplier=0,
                           allow_small_or_imprecise_dtypes=True).then_inc(consts, 1)

            words = [0]

            def wstep(ins):
                words[0] += 1
                ins.then_inc(word_step, 1)
                pool.wait_ge(word_step, words[0])

            pool.wait_ge(dst_loaded, 32 * len(edge_pieces()))
            nc.gpsimd.tensor_scalar(dst_w[:, :], dst_i[:, :], float(TYPES * BLOCK), float(-SHIFT), ALU.mult, ALU.add)
            wstep(nc.gpsimd.tensor_scalar(type_w[:, :], type_i[:, :], float(BLOCK), 0.0, ALU.mult, ALU.add))
            wstep(nc.gpsimd.tensor_tensor(word0[:, :], dst_w[:, :], type_w[:, :], ALU.add))
            pool.wait_ge(rows_ready, 1)
            wstep(nc.gpsimd.tensor_copy(row_w[:, :], row_i[:, :]))
            wstep(nc.gpsimd.tensor_tensor(word1[:, :], word0[:, :], row_w[:, :], ALU.add))
            wstep(nc.gpsimd.tensor_scalar(word_pos[:, :], word1[:, :], 0.0, None, ALU.is_ge))
            nc.gpsimd.tensor_tensor(word[:, :], word1[:, :], word_pos[:, :], ALU.add).then_inc(word_ready, 1)
            pool.wait_ge(word_ready, 1)


            pool.wait_ge(slots_zeroed, 16)
            pool.wait_ge(addr_ready, 1)

            def scatter_rounds(g, first):
                for half in range(2):
                    j = (g * 2 + half) * SU + PLACED
                    if not first:
                        pool.wait_ge(scattered[half], g * (16 * SU))
                    nc.gpsimd.tensor_copy(addr_ring[:, half, :], addr_i[:, bass.ds(j, SU)]).then_inc(addr_copied, 1)
                    nc.gpsimd.tensor_copy(word_ring[:, half, :], word[:, bass.ds(j, SU)]).then_inc(addr_copied, 1)
                    pool.wait_ge(addr_copied, g * 4 + 2 * (half + 1))
                    nc.gpsimd.nop(nofuse=True)
                    for s in range(SU):
                        nc.gpsimd.indirect_dma_start(
                            out=slots[:, :],
                            out_offset=bass.IndirectOffsetOnAxis(ap=addr_ring[:, half, s:s + 1], axis=0),
                            in_=word_ring[:, half, s:s + 1], in_offset=None).then_inc(scattered[half], 16)

            scatter_rounds(0, True)
            with pool.Fori(1, SCATTER_ROUNDS) as g:
                scatter_rounds(g, False)

            def gather(half, s):
                nc.gpsimd.indirect_dma_start(
                    out=gath[:, half, s, :], out_offset=None, in_=table[:, :],
                    in_offset=bass.IndirectOffsetOnAxis(ap=idx_ring[:, half, s:s + 1], axis=0)
                ).then_inc(gathered[half * GU + s], 16)

            for s in range(RY):
                pool.wait_ge(y_stored[s], 16 * len(range(s, NB, RY)))

            def gather_round(r, half):
                pool.wait_ge(idx_copied, r + 1)
                nc.gpsimd.nop(nofuse=True)
                for s in range(GU):
                    gather(half, s)

            gather_round(0, 0)
            gather_round(1, 1)
            with pool.Fori(1, TILES // RG) as g:
                for half in range(2):
                    gather_round(g * 2 + half, half)

        @block.scalar
        def _(act):
            act.dma_start(coef_bc[:, :, :].rearrange("p r b -> p (r b)"),
                          coefs.rearrange("r b -> (r b)").partition_broadcast(P)).then_inc(coef_loaded, 16)
            act.dma_start(bases_sb[:, :, :].rearrange("p h o -> p (h o)"),
                          bases.rearrange("b (i h) o -> (b i) (h o)", h=IH)).then_inc(bases_loaded, 16)
            load_edges(act, type_i, etype, dst_loaded)
            act.dma_start(wself[:, :], w_self[:, :]).then_inc(wself_loaded, 16)
            act.dma_start(x_sb[:, 0:NFULL, :], x[0:NFULL * P, :].rearrange("(q p) f -> p q f", p=P)).then_inc(x_loaded, 16)
            act.wait_ge(zero_ready, 2)
            act.dma_start(x_sb[0:NLAST, NFULL, :], x[NFULL * P:NODES, :]).then_inc(x_loaded, 16)

            for half in range(2):
                for c in range(2):
                    act.wait_ge(wmix_made, 2 * half + c + 1)
                    nc.scalar.copy(wmix[:, half, c * BANK:(c + 1) * BANK], ps[:, 2 * half + c, :]).then_inc(wmix_copied, 1)

            def next_x(q, s):
                nc.scalar.copy(xcur[:, s, :, :], xT[:, :, bass.ds(q, 1), :].rearrange("p d o n -> p d (o n)")).then_inc(xcur_ready, 1)

            for g in range(XG):
                n = min(4, NB - 4 * g)
                act.wait_ge(xT_made, g + 1)
                nc.scalar.copy(xT[:, 0, 4 * g:4 * g + n, :].rearrange("p q n -> p (q n)"),
                               ps[:, g, 0:n * P]).then_inc(xT_copied, 1)
            nc.scalar.copy(wselfT[:, :], ps[:, XG - 1, P:2 * P]).then_inc(xT_copied, 1)

            def digits(p, j, s, one):
                act.wait_ge(onehots_ready[p], j + 1)
                for d, digit in enumerate((hi_f, lo_f)):
                    last = nc.scalar.activation(slotoh[:, s, d, :], oneslot[:, one, :], ACT.Copy,
                                                scale=digit[:, bass.ds(j + p * SPLIT, 1)])
                last.then_inc(place_digits[p], 1)

            def copy_tile(q, s, n=None, ahead=True):
                for c in range(YC):
                    if n is not None and c == YC // 2:
                        turn = (s - EARLY) % RY
                        digits(0, n * YC + YC - 1, turn * YC + YC - 1, turn)
                    act.wait_ge(y_made, YC * q + c + 1)
                    nc.scalar.copy(ytile[:, s, c * BANK:(c + 1) * BANK], ps[:, c, :]).then_inc(y_copied, 1)
                if ahead:
                    next_x(q + 2, s % 2)

            act.wait_ge(x_low, 1)
            next_x(0, 0)
            next_x(1, 1)
            for c in range(YC):
                act.wait_ge(w_ready[c // 2], 16)
                bank = slice(c * BANK, (c + 1) * BANK)
                nc.scalar.copy(W_high[:, bank], W[:, bank]).then_inc(w_high, 1)
            act.wait_ge(x_low, XG)
            for q in range(RY):
                if q == RY - 2:
                    act.wait_ge(w_low, YC)
                copy_tile(q, q)
            with act.Fori(1, EARLY // RY) as g:
                for s in range(RY):
                    act.wait_ge(y_stored[s], g * 16)
                    copy_tile(g * RY + s, s)
            act.wait_ge(digits_ready, 1)
            for q in range(EARLY // RY * RY, (EARLY // RY + 1) * RY):
                act.wait_ge(y_stored[q % RY], 16 * (q // RY))
                copy_tile(q, q % RY, n=q - EARLY if q >= EARLY else None)
            with act.Fori(EARLY // RY + 1, NB // RY - 1) as g:
                for s in range(RY):
                    act.wait_ge(y_stored[s], g * 16)
                    copy_tile(g * RY + s, s, n=g * RY + s - EARLY)
            for q in range((NB // RY - 1) * RY, NB):
                act.wait_ge(y_stored[q % RY], 16 * (q // RY))
                copy_tile(q, q % RY, n=q - EARLY, ahead=q + 2 < NB)
            act.wait_ge(y_copied, YC * NB)
            act.dma_start(table.rearrange("(n t) o -> n (t o)", t=TYPES)[NFULL * P:NODES, :],
                          ytile[0:NLAST, NFULL % RY, :]).then_inc(y_stored[NFULL % RY], 16)

            with act.Fori(0, 2 * PLACE_PAIRS) as n:
                for v in ACT_DIGITS:
                    digits(1, n * PB + v, v, v)

            steps = [0]

            def step(ins):
                steps[0] += 1
                ins.then_inc(act_step, 1)
                act.wait_ge(act_step, steps[0])

            act.wait_ge(ends_ready, 1)
            act.wait_ge(self_added, NB)
            for y in y_stored:
                act.wait_ge(y, 16 * (NB // RY))
            for b in range(-(-NB // 4)):
                n = min(4, NB - 4 * b)
                if b < BLOCKS // 2:
                    done = act.value_load(ends_i[0:1, 2 * b + 1:2 * b + 2], min_val=TA, max_val=TILES)
                    act.wait_ge(summed, done)
                else:
                    act.wait_ge(summed, TILES)
                for q in range(4 * b, 4 * b + n):
                    last = nc.scalar.activation(h[:, q, :], acc[:, q * D:(q + 1) * D], ACT.Copy, accum_out=hsum[:, q:q + 1])
                step(last)
                step(nc.scalar.mul(hneg[:, 4 * b:4 * b + n], hsum[:, 4 * b:4 * b + n], -1.0 / D))
                for q in range(4 * b, 4 * b + n):
                    last = nc.scalar.activation(sq[:, q % 4, :], h[:, q, :], ACT.Square, bias=hneg[:, q:q + 1],
                                                accum_out=hvar[:, q:q + 1])
                step(last)
                nc.scalar.activation(hstd[:, 4 * b:4 * b + n], hvar[:, 4 * b:4 * b + n], ACT.Sqrt, bias=eps_c[:, 0:1],
                                     scale=1.0 / D).then_inc(std_ready, 1)

        @block.vector
        def _(dve):
            steps = [0]

            def step(ins):
                steps[0] += 1
                ins.then_inc(dve_step, 1)
                dve.wait_ge(dve_step, steps[0])

            nc.vector.memset(zeros[:, :], 0.0).then_inc(zero_ready, 1)
            nc.vector.memset(x_sb[:, NFULL, :], 0.0).then_inc(zero_ready, 1)
            nc.vector.memset(zeros_h[:, :], 0.0).then_inc(zero_ready, 1)
            nc.vector.memset(ones_row[:, :], 1.0)
            nc.vector.memset(eps_c[:, :], EPS)
            nc.vector.memset(tile_f[:, EJ:EJB], -1.0)
            for blank in (slot_f, hi_f, lo_f):
                nc.vector.memset(blank[:, EJ:EJB], 0.0)
            nc.vector.memset(ones[:, :], 1.0).then_inc(masks, 1)
            dve.wait_ge(consts, CONSTS)
            nc.vector.tensor_scalar(ident[:, :], diag[:, :], 0.0, None, ALU.is_equal).then_inc(masks, 1)
            nc.vector.tensor_scalar(before[:, :], diag[:, :], 0.0, None, ALU.is_gt).then_inc(masks, 1)
            dve.wait_ge(masks, 3)

            nc.vector.tensor_scalar(own_s[:, :], own_i[:, :], IC.bit_length() - 1, None, ALU.arith_shift_right)
            step(nc.vector.tensor_scalar(same_m[:, :], same_i[:, :], IC - 1, None, ALU.bitwise_and))
            nc.vector.tensor_scalar(own[:, :], own_s[:, :], 0.0, None, ALU.is_equal)
            step(nc.vector.tensor_scalar(same[:, :], same_m[:, :], 0.0, None, ALU.is_equal))
            dve.wait_ge(coef_loaded, 16)
            step(nc.vector.tensor_tensor(coef_own[:, :, :], coef_bc[:, :, :], own[:, :].unsqueeze(1).broadcast_to([P, TYPES, BASES]),
                                         ALU.mult))
            step(nc.vector.tensor_reduce(coef_col[:, :], coef_own[:, :, :], AX_X, ALU.add))
            nc.vector.tensor_tensor(mix[:, :, :], coef_col[:, :].unsqueeze(2).broadcast_to([P, TYPES, IC]),
                                    same[:, :].unsqueeze(1).broadcast_to([P, TYPES, IC]), ALU.mult).then_inc(mix_ready, 1)

            dve.wait_ge(src_loaded, 16 * len(edge_pieces()))
            nc.vector.tensor_scalar(row_i[:, :], src_i[:, :], BLOCK - 1, None, ALU.bitwise_and).then_inc(rows_ready, 1)
            step(nc.vector.tensor_scalar(blk_i[:, :], src_i[:, :], BLOCK.bit_length() - 1, None, ALU.arith_shift_right))
            step(nc.vector.tensor_copy(blk_h[:, :], blk_i[:, :]))

            def in_block(lo, hi):
                for k in range(BLOCKS):
                    last = nc.vector.tensor_scalar(inblk[:, k, lo:hi], blk_h[:, lo:hi], float(k), None, ALU.is_equal)
                step(last)

            def scan(lo, hi):
                for k in range(BLOCKS):
                    last = nc.vector.tensor_tensor_scan(rank[:, k, lo:hi], ones_row[0:EP, lo:hi], inblk[:, k, lo:hi], 0.0,
                                                        ALU.mult, ALU.add)
                last.then_inc(ranks_ready, 1)

            def block_starts(p):
                dve.wait_ge(prefix_ready, p + 1)
                step(nc.vector.tensor_scalar(need_i[:, p, :], ps_total[p], float(P - 1), None, ALU.add))
                step(nc.vector.tensor_scalar(need_t[:, p, :], need_i[:, p, :], P.bit_length() - 1, None, ALU.arith_shift_right))
                step(nc.vector.tensor_copy(need_f[:, p, :], need_t[:, p, :]))
                step(nc.vector.tensor_tensor_scan(ends[:, p, :], ones_row[:, 0:BLOCKS], need_f[:, p, :], 0.0, ALU.mult, ALU.add))
                step(nc.vector.tensor_tensor(starts[:, p, :], ends[:, p, :], need_f[:, p, :], ALU.subtract))
                step(nc.vector.scalar_tensor_tensor(offs[:, p, :], starts[0:EP, p, :], float(P), ps_before[p], ALU.mult, ALU.add))

            def sorted_slots(p, lo, hi):
                for k in range(BLOCKS):
                    last = nc.vector.scalar_tensor_tensor(rank[:, k, lo:hi], rank[:, k, lo:hi], offs[:, p, k:k + 1],
                                                          inblk[:, k, lo:hi], ALU.add, ALU.mult)
                step(last)
                step(nc.vector.tensor_reduce(pos_f[:, lo:hi], rank[:, :, lo:hi].rearrange("p k j -> p j k"), AX_X, ALU.add))
                step(nc.vector.tensor_scalar(pos_i[:, lo:hi], pos_f[:, lo:hi], -1.0, None, ALU.add))
                nc.vector.tensor_scalar(tile_i[:, lo:hi], pos_i[:, lo:hi], P.bit_length() - 1, None, ALU.arith_shift_right)
                step(nc.vector.tensor_scalar(slot_i[:, lo:hi], pos_i[:, lo:hi], P - 1, None, ALU.bitwise_and))

            def slots_to_float(lo, hi):
                nc.vector.tensor_copy(tile_f[:, lo:hi], tile_i[:, lo:hi])
                step(nc.vector.tensor_copy(slot_f[:, lo:hi], slot_i[:, lo:hi]))

            def x_low_part(g):
                tiles = slice(4 * g, min(4 * g + 4, NB))
                n = (tiles.stop - tiles.start) * P
                dve.wait_ge(xT_copied, g + 1)
                nc.vector.tensor_tensor(xT[:, 1, tiles, :].rearrange("p q n -> p (q n)"), ps[:, g, 0:n],
                                        xT[:, 0, tiles, :].rearrange("p q n -> p (q n)"), ALU.subtract).then_inc(x_low, 1)

            in_block(0, SPLIT)
            scan(0, SPLIT)
            block_starts(0)
            sorted_slots(0, PLACED, SPLIT)
            nc.vector.scalar_tensor_tensor(addr_i[:, PLACED:SPLIT], slot_i[:, PLACED:SPLIT], float(TA), tile_i[:, PLACED:SPLIT],
                                           ALU.mult, ALU.add).then_inc(addr_ready, 1)

            for g in range(YC):
                x_low_part(g)
            for c in range(YC):
                dve.wait_ge(w_high, c + 1)
                bank = slice(c * BANK, (c + 1) * BANK)
                nc.vector.tensor_tensor(W_low[:, bank], W[:, bank], W_high[:, bank], ALU.subtract).then_inc(w_low, 1)
            for g in range(YC, XG):
                x_low_part(g)

            in_block(SPLIT, EJ)
            scan(SPLIT, EJ)
            sorted_slots(0, 0, PLACED)
            slots_to_float(0, PLACED)

            dve.wait_ge(word_ready, 1)
            step(nc.vector.tensor_scalar(wdig_i[:, :], word[:, :], float(DIGIT // 2), None, ALU.add))
            nc.vector.tensor_scalar(hi_i[:, :], wdig_i[:, :], DIGIT.bit_length() - 1, None, ALU.arith_shift_right)
            step(nc.vector.tensor_scalar(lo_i[:, :], wdig_i[:, :], DIGIT - 1, None, ALU.bitwise_and))
            nc.vector.tensor_copy(hi_f[:, 0:EJ], hi_i[:, :])
            nc.vector.tensor_scalar(lo_f[:, 0:EJ], lo_i[:, :], float(-DIGIT // 2), None, ALU.add).then_inc(digits_ready, 1)
            dve.wait_ge(digits_ready, 1)

            block_starts(1)
            sorted_slots(1, SPLIT, EJ)
            slots_to_float(SPLIT, EJ)

            def count_ends(p, n, blocks):
                for k in blocks:
                    if k == 0:
                        step(nc.vector.tensor_scalar(tblk[0][:, 0:n], iota_t1[:, 0:n], ends[0:1, p, 0:1], None, ALU.is_ge))
                    else:
                        step(nc.vector.scalar_tensor_tensor(tblk[k % 2][:, 0:n], iota_t1[:, 0:n], ends[0:1, p, k:k + 1],
                                                            tblk[(k - 1) % 2][:, 0:n], ALU.is_ge, ALU.add))

            def block_columns(first, n):
                nc.vector.tensor_scalar(tblk_i[:, first:first + n], tblk[(BLOCKS - 2) % 2][:, 0:n], float(BLOCK), None,
                                        ALU.mult).then_inc(tblk_ready, 1)

            def place(p, j, s, dve_digits):
                slot = slot_f[:, bass.ds(j + p * SPLIT, 1)]
                if dve_digits:
                    for d, digit in enumerate((hi_f, lo_f)):
                        nc.vector.tensor_scalar(slotoh[:, s, d, :], iota_slot[0:EP, :], slot, digit[:, bass.ds(j + p * SPLIT, 1)],
                                                ALU.is_equal, ALU.mult)
                else:
                    nc.vector.tensor_scalar(oneslot[:, s if p else s // YC, :], iota_slot[0:EP, :], slot, None, ALU.is_equal)
                n = (TA, TB)[p]
                nc.vector.tensor_scalar(tileoh[:, s, 0:n], iota_tile[0:EP, 0:n], tile_f[:, bass.ds(j + p * SPLIT, 1)], None,
                                        ALU.is_equal).then_inc(onehots_ready[p], 1)

            for j in range(RP):
                place(0, j, j, j % YC != YC - 1)
            nc.vector.tensor_scalar(ends_i[:, :], ends[0:1, 1, :], float(TA), None, ALU.add).then_inc(ends_ready, 1)

            def place_rounds(first, end):
                with dve.Fori(first, end) as g:
                    for s in range(RP):
                        j = g * RP + s
                        dve.wait_ge(place_used[0], j - (RP - 1))
                        place(0, j, s, s % YC != YC - 1)

            place_rounds(1, 2)
            count_ends(0, TA, range(BLOCKS - 1))
            block_columns(0, TA)
            place_rounds(2, GROUPS * YC // RP)
            for j in range(GROUPS * YC // RP * RP, PLACED):
                dve.wait_ge(place_used[0], j - (RP - 1))
                place(0, j, j % RP, j >= GROUPS * YC or j % YC != YC - 1)

            reads = [0]

            def table_rows(p, lo, hi):
                first = p * TA
                hi_sum, lo_sum = [a[:, lo - first:hi - first] for a in ps_digits[p]]
                if p == 0:
                    step(nc.vector.scalar_tensor_tensor(sw0[:, lo:hi], hi_sum, float(DIGIT), sD[:, lo:hi], ALU.mult, ALU.add))
                else:
                    step(nc.vector.tensor_scalar(sw0[:, lo:hi], hi_sum, float(DIGIT), None, ALU.mult))
                nc.vector.tensor_tensor(sw[:, lo:hi], lo_sum, sw0[:, lo:hi], ALU.add).then_inc(slots_read, 1)
                reads[0] += 1
                dve.wait_ge(slots_read, reads[0])
                step(nc.vector.scalar_tensor_tensor(sneg[:, lo:hi], sw[:, lo:hi], 0.0, sw[:, lo:hi], ALU.is_gt, ALU.subtract))
                step(nc.vector.tensor_scalar(sval[:, lo:hi], sneg[:, lo:hi], -1.0, float(SHIFT), ALU.mult, ALU.add))
                step(nc.vector.tensor_scalar(sidx[:, lo:hi], sval[:, lo:hi], BLOCK.bit_length() - 1, None, ALU.arith_shift_right))

            def rows_in_block(lo, hi):
                nc.vector.tensor_scalar(sempty[:, lo:hi], sw[:, lo:hi], 0.0, float(2 * BLOCK), ALU.is_equal, ALU.mult)
                step(nc.vector.tensor_scalar(srow_i[:, lo:hi], sval[:, lo:hi], BLOCK - 1, None, ALU.bitwise_and))
                step(nc.vector.tensor_tensor(srow[:, lo:hi], srow_i[:, lo:hi], sempty[:, lo:hi], ALU.add))

            def copy_indices(r, half):
                nc.vector.tensor_copy(idx_ring[:, half, :], sidx[:, bass.ds(r * GU, GU)]).then_inc(idx_copied, 1)

            def row_onehot(t, s):
                nc.vector.tensor_scalar(rowoh[:, s, :], iota_row[:, :], srow[:, bass.ds(t, 1)], None,
                                        ALU.is_equal).then_inc(rowoh_ready, 1)

            dve.wait_ge(place_used[0], PLACED)
            dve.wait_ge(slots_loaded, 16)
            table_rows(0, 0, RG)
            for half in range(2):
                copy_indices(half, half)
            table_rows(0, RG, TA)
            rows_in_block(0, TA)

            def place_share(n, i, first):
                for v in share(i):
                    if not first:
                        dve.wait_ge(place_used[1], n * PB + v - (PB - 1))
                    place(1, n * PB + v, v, v in DVE_DIGITS)

            def round_operands(r, half, group=None):
                for i in range(GU):
                    if group is not None:
                        place_share(group, i, False)
                    if i == 1:
                        dve.wait_ge(summed, r * GU - GU)
                        copy_indices(r, half)
                        row_onehot(r * GU, half * GU)
                    if i >= 1:
                        row_onehot(r * GU + i, half * GU + i)

            for t in range(GU):
                row_onehot(t, t)
            for i in range(GU):
                row_onehot(GU + i, GU + i)
                place_share(0, i, True)

            def whole(q, n):
                nc.vector.tensor_tensor(xT_whole[:, bass.ds(q, n), :], xT[:, 0, bass.ds(q, n), :], xT[:, 1, bass.ds(q, n), :],
                                        ALU.add).then_inc(x_whole, 1)

            share_of_x = NFULL // (PLACE_PAIRS - 1)
            with dve.Fori(1, PLACE_PAIRS) as g:
                for half in range(2):
                    round_operands(g * 2 + half, half, group=g * 2 + half - 1)
                whole(g * share_of_x - share_of_x, share_of_x)
            whole(NFULL, 1)
            round_operands(2 * PLACE_PAIRS, 0, group=2 * PLACE_PAIRS - 1)
            round_operands(2 * PLACE_PAIRS + 1, 1)

            dve.wait_ge(place_used[1], 2 * PLACE_PAIRS * PB)
            table_rows(1, TA, TILES)
            rows_in_block(TA, TILES)
            count_ends(1, TB, range(0, BLOCKS // 2))
            round_operands(2 * PLACE_PAIRS + 2, 0)
            count_ends(1, TB, range(BLOCKS // 2, BLOCKS - 1))
            block_columns(TA, TB)
            round_operands(2 * PLACE_PAIRS + 3, 1)
            with dve.Fori(PLACE_PAIRS + 2, TILES // RG) as g:
                for half in range(2):
                    round_operands(g * 2 + half, half)

            def normalise(first, end, banks, parts):
                dve.wait_ge(std_ready, banks)
                step(nc.vector.reciprocal(hinv[:, first:end], hstd[:, first:end]))
                for q in range(first, end):
                    last = nc.vector.tensor_scalar(normal[:, q, :], h[:, q, :], hneg[:, q:q + 1], hinv[:, q:q + 1],
                                                   ALU.add, ALU.mult)
                    if (q + 1 - first) % ((end - first) // parts) == 0:
                        last.then_inc(normed, 1)

            normalise(0, NFULL, NFULL // 4, 2)
            normalise(NFULL, NB, NFULL // 4 + 1, 1)

        @block.tensor
        def _(pe):
            def keep_warm(n):
                for _ in range(n):
                    nc.tensor.matmul(ps[:, 7, 0:EJ], zeros_h[:, 0:P], zeros_h[:, 0:EJ], start=True, stop=True)

            pe.wait_ge(zero_ready, 3)
            keep_warm(WARM[0])

            def prefix(p):
                pe.wait_ge(ranks_ready, p + 1)
                last = rank[:, :, (SPLIT, EJ)[p] - 1]
                nc.tensor.matmul(ps_before[p], before[0:EP, 0:EP], last, start=True, stop=True)
                nc.tensor.matmul(ps_total[p], ones[0:EP, :], last, start=True, stop=True).then_inc(prefix_ready, 1)

            pe.wait_ge(mix_ready, 1)
            pe.wait_ge(bases_loaded, 16)
            for half in range(2):
                for c in range(2):
                    nc.tensor.matmul(ps[:, 2 * half + c, :],
                                     mix[:, half * TYPES // 2:(half + 1) * TYPES // 2, :].rearrange("p r i -> p (r i)"),
                                     bases_sb[:, c * IH // 2:(c + 1) * IH // 2, :].rearrange("p h o -> p (h o)"),
                                     start=True, stop=True).then_inc(wmix_made, 1)

            pe.wait_ge(masks, 3)
            prefix(0)

            pe.wait_ge(x_loaded, 32)
            for g in range(XG):
                n = min(4, NB - 4 * g)
                if g < YC:
                    pe.wait_ge(wmix_copied, g + 1)
                for i in range(n):
                    last = nc.tensor.transpose(ps[:, g, i * P:(i + 1) * P], x_sb[:, 4 * g + i, :], ident[:, :])
                if g == XG - 1:
                    pe.wait_ge(wself_loaded, 16)
                    last = nc.tensor.transpose(ps[:, g, P:2 * P], wself[:, :], ident[:, :])
                last.then_inc(xT_made, 1)

            def table_bank(q, s, c, first=False):
                if first:
                    pe.wait_ge(x_low, c + 1)
                    pe.wait_ge(w_low, c + 1)
                else:
                    pe.wait_ge(y_copied, YC * q + c - (YC - 1))
                bank = slice(c * BANK, (c + 1) * BANK)
                nc.tensor.matmul(ps[:, c, :], xcur[:, s, 0, :], W_high[:, bank], start=True, stop=False)
                nc.tensor.matmul(ps[:, c, :], xcur[:, s, 0, :], W_low[:, bank], start=False, stop=False)
                nc.tensor.matmul(ps[:, c, :], xcur[:, s, 1, :], W_high[:, bank], start=False, stop=True).then_inc(y_made, 1)

            def table_tile(q, s):
                pe.wait_ge(xcur_ready, q + 1)
                for c in range(YC):
                    table_bank(q, s, c)

            pe.wait_ge(addr_ready, 1)
            keep_warm(WARM[1])
            pe.wait_ge(xcur_ready, 1)
            for c in range(YC):
                table_bank(0, 0, c, first=True)

            def table_tiles(first, end):
                with pe.Fori(0, (end - first) // 2) as g:
                    for u in range(2):
                        table_tile(g * 2 + first + u, (first + u) % 2)
                if (end - first) % 2:
                    table_tile(end - 1, (end - 1) % 2)

            table_tiles(1, BEFORE_PREFIX)
            prefix(1)
            table_tiles(BEFORE_PREFIX, EARLY)

            pe.wait_ge(x_low, XG)
            nc.tensor.matmul(ps[:, 4, :], zeros_h[:, 0:P], zeros_h[:, :], start=True, stop=False, skip_group_check=True)

            def place(p, s):
                for d in range(2):
                    last = nc.tensor.matmul(ps_digits[p][d], slotoh[:, s, d, :], tileoh[:, s, 0:(TA, TB)[p]], start=False,
                                            stop=False, skip_group_check=True)
                last.then_inc(place_used[p], 1)

            def table_tile_and_placings(q, s, n, s0):
                pe.wait_ge(xcur_ready, q + 1)
                for c in range(YC):
                    table_bank(q, s, c)
                    if c < YC - 1:
                        pe.wait_ge(onehots_ready[0], n * YC + c + 1)
                    else:
                        pe.wait_ge(place_digits[0], n + 1)
                    place(0, s0 + c)

            per = RP // YC
            with pe.Fori(0, GROUPS // per) as g:
                for u in range(per):
                    table_tile_and_placings(g * per + EARLY + u, (EARLY + u) % 2, g * per + u, u * YC)
            for n in range(GROUPS // per * per, GROUPS):
                table_tile_and_placings(EARLY + n, (EARLY + n) % 2, n, n % per * YC)
            for j in range(GROUPS * YC, PLACED):
                pe.wait_ge(onehots_ready[0], j + 1)
                place(0, j % RP)

            pe.wait_ge(y_copied, YC * NB)
            for bank in (0, 1, 2, 3, 5, 6, 4):
                if bank == 4:
                    pe.wait_ge(slots_read, 2)
                nc.tensor.matmul(ps[:, bank, :], zeros_h[:, 0:P], zeros_h[:, :], start=True, stop=False, skip_group_check=True)

            def add_self(q):
                for rows in (wselfT, ident):
                    last = nc.tensor.matmul(acc[:, q * P:(q + 1) * P], xT_whole[:, q, :], rows[:, :], start=False, stop=False,
                                            skip_group_check=True)
                last.then_inc(self_added, 1)

            def block_columns(t, n):
                _, cols = nc.values_load_multi_w_load_instructions(
                    tblk_i[0:1, bass.ds(t, n)], engines=[mybir.EngineType.PE], min_val=0, max_val=(BLOCKS - 1) * BLOCK,
                    skip_runtime_bounds_check_because="it is a count of up to BLOCKS - 1 blocks times BLOCK")
                return cols

            def add_tile(g, s, col):
                t = g * RG + s
                pe.wait_ge(rowoh_ready, t + 1)
                pe.wait_ge(gathered[s], 16 * (g + 1))
                for c in range(BLOCK // P):
                    last = nc.tensor.matmul(acc[:, bass.ds(col + c * P, P)], rowoh[:, s, c * P:(c + 1) * P],
                                            gath[:, s // GU, s % GU, :], start=False, stop=False, skip_group_check=True)
                last.then_inc(summed, 1)

            def place_share(n, i):
                for v in share(i):
                    if v in DVE_DIGITS:
                        pe.wait_ge(onehots_ready[1], n * PB + v + 1)
                    else:
                        pe.wait_ge(place_digits[1], n * len(ACT_DIGITS) + ACT_DIGITS.index(v) + 1)
                    place(1, v)

            pe.wait_ge(ends_ready, 1)
            pe.wait_ge(tblk_ready, 1)
            nc.tensor.matmul(ps[:, 7, :], zeros_h[:, 0:P], zeros_h[:, :], start=True, stop=False, skip_group_check=True)
            with pe.Fori(0, PLACE_PAIRS) as g:
                for half in range(2):
                    for i, col in enumerate(block_columns(g * RG + half * GU, GU)):
                        add_tile(g, half * GU + i, col)
                        place_share(g * 2 + half, i)

            def pair_of_rounds(g, and_self=None):
                for half in range(2):
                    for i, col in enumerate(block_columns(g * RG + half * GU, GU)):
                        add_tile(g, half * GU + i, col)
                        if and_self is not None:
                            done = and_self * RG + half * GU + i
                            for q in range(done * NB // (SELF_PAIRS * RG), (done + 1) * NB // (SELF_PAIRS * RG)):
                                add_self(q)

            pe.wait_ge(x_whole, PLACE_PAIRS)
            pe.wait_ge(xT_copied, XG + 1)
            for i in range(SELF_PAIRS):
                if PLACE_PAIRS + i == TA // RG:
                    pe.wait_ge(tblk_ready, 2)
                pair_of_rounds(PLACE_PAIRS + i, and_self=i)
            with pe.Fori(PLACE_PAIRS + SELF_PAIRS, TILES // RG) as g:
                pair_of_rounds(g)


def kernel(x, src, dst, edge_type_16, L0_gnn_bases, L0_gnn_coefficients, L0_gnn_w_self):
    import numpy as np
    import concourse.bacc as bacc
    from concourse.bass_utils import run_bass_kernel_spmd

    nc = bacc.Bacc("TRN2", target_bir_lowering=False, num_devices=1)
    named = dict(x=x, src=src, dst=dst, etype=edge_type_16, bases=L0_gnn_bases, coefs=L0_gnn_coefficients,
                 w_self=L0_gnn_w_self)
    arrays, args = {}, []
    for name, a in named.items():
        a = np.ascontiguousarray(a)
        arrays[f"in_{name}"] = a
        args.append(nc.dram_tensor(f"in_{name}", a.shape, mybir.dt.from_np(a.dtype), kind="ExternalInput").ap())
    out = nc.dram_tensor("out_0", (NODES, D), F32, kind="ExternalOutput").ap()
    rgcn(nc, *args, out)
    r = run_bass_kernel_spmd(nc, [arrays], core_ids=[0])
    return r.results[0]["out_0"]
```
